# Optimizing a Trainium2 kernel written in Bass

```python
import numpy as np
import jax
import jax.numpy as jnp

def _softmax(x, axis=-1):
    return jax.nn.softmax(x, axis=axis)

def _gelu(x):
    return jax.nn.gelu(x, approximate=True)

def _silu(x):
    return jax.nn.silu(x)

def _sigmoid(x):
    return jax.nn.sigmoid(x)

def _layernorm(x, axis=-1, eps=1e-05):
    m = jnp.mean(x, axis=axis, keepdims=True)
    v = jnp.var(x, axis=axis, keepdims=True)
    return (x - m) / jnp.sqrt(v + eps)

def _scatter_add(tgt, idx, src, axis=0):
    return tgt.at[idx].add(src)

def _segment_sum(src, seg, n):
    return jax.ops.segment_sum(src, seg, n)
kernel_name = 'mk_prb_d1_jaxref_r4_5be171'

def setup_inputs(seed: int=0):
    np.random.seed(seed)
    _w = jnp.asarray

    def _L0_attn_setup():
        import jax, jax.numpy as jnp
        import numpy as np
        D_MODEL = 256
        NUM_HEADS = 16
        D_K = D_MODEL // NUM_HEADS
        BATCH, SEQ = (2, 512)
        key = jax.random.key(seed)
        k = jax.random.split(key, 5)
        std = np.sqrt(2.0 / (D_MODEL + D_MODEL)).astype(np.float32)
        return {'x': jax.random.normal(k[0], (BATCH, SEQ, D_MODEL), dtype=jnp.float32), 'WQ': jax.random.normal(k[1], (D_MODEL, D_MODEL), dtype=jnp.float32) * std, 'WK': jax.random.normal(k[2], (D_MODEL, D_MODEL), dtype=jnp.float32) * std, 'WV': jax.random.normal(k[3], (D_MODEL, D_MODEL), dtype=jnp.float32) * std, 'WO': jax.random.normal(k[4], (D_MODEL, D_MODEL), dtype=jnp.float32) * std}
    _L0_attn_in = _L0_attn_setup()

    def _L0_ffn_setup():
        import jax, jax.numpy as jnp
        import numpy as np
        D, H, P, E, K, F = (256, 16, 64, 8, 2, 1024)
        B, S = (2, 512)
        NROT = 32
        BASE = 10000.0
        EPS = 1e-05

        def _ln(x, g, b):
            m = jnp.mean(x, -1, keepdims=True)
            v = jnp.mean(jnp.square(x - m), -1, keepdims=True)
            return (x - m) * jax.lax.rsqrt(v + EPS) * g + b

        def _rope(x):
            xr, xp = (x[..., :NROT], x[..., NROT:])
            half = NROT // 2
            inv = BASE ** (-jnp.arange(half, dtype=jnp.float32) / half)
            ang = jnp.arange(x.shape[2], dtype=jnp.float32)[:, None] * inv[None, :]
            cos, sin = (jnp.cos(ang), jnp.sin(ang))
            x1, x2 = (xr[..., :half], xr[..., half:])
            xr = jnp.concatenate([x1 * cos - x2 * sin, x1 * sin + x2 * cos], -1)
            return jnp.concatenate([xr, xp], -1)

        def _gate(x, Wsel):
            s = jax.nn.sigmoid(jnp.einsum('bsd,hed->bhse', x, Wsel))
            _, idx = jax.lax.top_k(s, K)
            mask = jax.nn.one_hot(idx, E, dtype=s.dtype).sum(-2)
            return s * mask

        def _moe_attn(x, Wq, Wk, Wv, Wo, Wsel_v, Wsel_o):
            q = _rope(jnp.einsum('bsd,hdp->bhsp', x, Wq))
            k = _rope(jnp.einsum('bsd,hdp->bhsp', x, Wk))
            gv = _gate(x, Wsel_v)
            v = jnp.einsum('bsd,bhse,hedp->bhsp', x, gv, Wv)
            att = jax.nn.softmax(jnp.einsum('bhsp,bhtp->bhst', q, k) / np.sqrt(P), axis=-1)
            o = jnp.einsum('bhst,bhtp->bhsp', att, v)
            go = _gate(x, Wsel_o)
            return jnp.einsum('bhsp,bhse,hepd->bsd', o, go, Wo)
        key = jax.random.key(seed)
        ks = jax.random.split(key, 10)
        f = lambda k, sh: jax.random.normal(k, sh, jnp.float32) * 0.02
        return dict(src=jax.random.normal(ks[0], (B, S, D), jnp.float32), Wq=f(ks[1], (H, D, P)), Wk=f(ks[2], (H, D, P)), Wv=f(ks[3], (H, E, D, P)), Wo=f(ks[4], (H, E, P, D)), Wsel_v=f(ks[5], (H, E, D)), Wsel_o=f(ks[6], (H, E, D)), ln1_g=jnp.ones(D, jnp.float32), ln1_b=jnp.zeros(D, jnp.float32), ln2_g=jnp.ones(D, jnp.float32), ln2_b=jnp.zeros(D, jnp.float32), W1=f(ks[7], (D, F)), b1=jnp.zeros(F, jnp.float32), W2=f(ks[8], (F, D)), b2=jnp.zeros(D, jnp.float32))
    _L0_ffn_in = _L0_ffn_setup()
    _d = {'L0_attn_x': _L0_attn_in['x'], 'L0_attn_WQ': _L0_attn_in['WQ'], 'L0_attn_WK': _L0_attn_in['WK'], 'L0_attn_WV': _L0_attn_in['WV'], 'L0_attn_WO': _L0_attn_in['WO'], 'L0_ffn_Wq': _L0_ffn_in['Wq'], 'L0_ffn_Wk': _L0_ffn_in['Wk'], 'L0_ffn_Wv': _L0_ffn_in['Wv'], 'L0_ffn_Wo': _L0_ffn_in['Wo'], 'L0_ffn_Wsel_v': _L0_ffn_in['Wsel_v'], 'L0_ffn_Wsel_o': _L0_ffn_in['Wsel_o'], 'L0_ffn_ln1_g': _L0_ffn_in['ln1_g'], 'L0_ffn_ln1_b': _L0_ffn_in['ln1_b'], 'L0_ffn_ln2_g': _L0_ffn_in['ln2_g'], 'L0_ffn_ln2_b': _L0_ffn_in['ln2_b'], 'L0_ffn_W1': _L0_ffn_in['W1'], 'L0_ffn_b1': _L0_ffn_in['b1'], 'L0_ffn_W2': _L0_ffn_in['W2'], 'L0_ffn_b2': _L0_ffn_in['b2']}
    _x0 = _d['L0_attn_x']
    _d['L0_attn_x'] = jax.random.normal(jax.random.fold_in(jax.random.key(seed), 1), (8, 512, 256), dtype=_x0.dtype)
    del _x0
    return _d

def reference(L0_attn_x, L0_attn_WQ, L0_attn_WK, L0_attn_WV, L0_attn_WO, L0_ffn_Wq, L0_ffn_Wk, L0_ffn_Wv, L0_ffn_Wo, L0_ffn_Wsel_v, L0_ffn_Wsel_o, L0_ffn_ln1_g, L0_ffn_ln1_b, L0_ffn_ln2_g, L0_ffn_ln2_b, L0_ffn_W1, L0_ffn_b1, L0_ffn_W2, L0_ffn_b2):

    def _L0_attn_ref(x, WQ, WK, WV, WO):
        import jax, jax.numpy as jnp
        import numpy as np
        D_MODEL = 256
        NUM_HEADS = 16
        D_K = D_MODEL // NUM_HEADS
        BATCH, SEQ = (2, 512)
        B, S, E = x.shape
        mask = jnp.where(jnp.triu(jnp.ones((S, S), dtype=bool), k=1), -jnp.inf, 0.0).astype(x.dtype)

        def heads(W):
            return (x @ W).reshape(B, S, NUM_HEADS, D_K).transpose(0, 2, 1, 3)
        Q, K, V = (heads(WQ), heads(WK), heads(WV))
        score = jnp.einsum('bhqd,bhkd->bhqk', Q, K) / jnp.sqrt(jnp.asarray(D_K, x.dtype))
        score = score + mask
        score = score - jnp.max(score, axis=-1, keepdims=True)
        score = jnp.exp(score)
        score = score / jnp.sum(score, axis=-1, keepdims=True)
        out = jnp.einsum('bhqk,bhkd->bhqd', score, V)
        out = out.transpose(0, 2, 1, 3).reshape(B, S, E)
        return out @ WO

    def _L0_ffn_ref(src, Wq, Wk, Wv, Wo, Wsel_v, Wsel_o, ln1_g, ln1_b, ln2_g, ln2_b, W1, b1, W2, b2):
        import jax, jax.numpy as jnp
        import numpy as np
        D, H, P, E, K, F = (256, 16, 64, 8, 2, 1024)
        B, S = (2, 512)
        NROT = 32
        BASE = 10000.0
        EPS = 1e-05

        def _ln(x, g, b):
            m = jnp.mean(x, -1, keepdims=True)
            v = jnp.mean(jnp.square(x - m), -1, keepdims=True)
            return (x - m) * jax.lax.rsqrt(v + EPS) * g + b

        def _rope(x):
            xr, xp = (x[..., :NROT], x[..., NROT:])
            half = NROT // 2
            inv = BASE ** (-jnp.arange(half, dtype=jnp.float32) / half)
            ang = jnp.arange(x.shape[2], dtype=jnp.float32)[:, None] * inv[None, :]
            cos, sin = (jnp.cos(ang), jnp.sin(ang))
            x1, x2 = (xr[..., :half], xr[..., half:])
            xr = jnp.concatenate([x1 * cos - x2 * sin, x1 * sin + x2 * cos], -1)
            return jnp.concatenate([xr, xp], -1)

        def _gate(x, Wsel):
            s = jax.nn.sigmoid(jnp.einsum('bsd,hed->bhse', x, Wsel))
            _, idx = jax.lax.top_k(s, K)
            mask = jax.nn.one_hot(idx, E, dtype=s.dtype).sum(-2)
            return s * mask

        def _moe_attn(x, Wq, Wk, Wv, Wo, Wsel_v, Wsel_o):
            q = _rope(jnp.einsum('bsd,hdp->bhsp', x, Wq))
            k = _rope(jnp.einsum('bsd,hdp->bhsp', x, Wk))
            gv = _gate(x, Wsel_v)
            v = jnp.einsum('bsd,bhse,hedp->bhsp', x, gv, Wv)
            att = jax.nn.softmax(jnp.einsum('bhsp,bhtp->bhst', q, k) / np.sqrt(P), axis=-1)
            o = jnp.einsum('bhst,bhtp->bhsp', att, v)
            go = _gate(x, Wsel_o)
            return jnp.einsum('bhsp,bhse,hepd->bsd', o, go, Wo)
        src2 = _moe_attn(src, Wq, Wk, Wv, Wo, Wsel_v, Wsel_o)
        src = src + src2
        src = _ln(src, ln1_g, ln1_b)
        src2 = jax.nn.relu(src @ W1 + b1) @ W2 + b2
        src = src + src2
        return _ln(src, ln2_g, ln2_b)
    x = L0_attn_x
    xn = _layernorm(x, axis=-1)
    x = x + _L0_attn_ref(xn, L0_attn_WQ, L0_attn_WK, L0_attn_WV, L0_attn_WO) + _L0_ffn_ref(xn, L0_ffn_Wq, L0_ffn_Wk, L0_ffn_Wv, L0_ffn_Wo, L0_ffn_Wsel_v, L0_ffn_Wsel_o, L0_ffn_ln1_g, L0_ffn_ln1_b, L0_ffn_ln2_g, L0_ffn_ln2_b, L0_ffn_W1, L0_ffn_b1, L0_ffn_W2, L0_ffn_b2)
    return x

_drawn_inputs = setup_inputs


def setup_inputs(seed=0):
    import zlib

    import numpy as np

    out = dict(_drawn_inputs(seed))
    spreads = {'L0_ffn_ln1_g': (1.0, 0.2),
     'L0_ffn_ln1_b': (0.0, 0.1),
     'L0_ffn_ln2_g': (1.0, 0.2),
     'L0_ffn_ln2_b': (0.0, 0.1),
     'L0_ffn_b1': (0.0, 0.4),
     'L0_ffn_b2': (0.0, 0.1)}
    factors = {'L0_ffn_Wq': 8.0,
     'L0_ffn_Wk': 8.0,
     'L0_ffn_Wv': 8.0,
     'L0_ffn_Wo': 8.0,
     'L0_ffn_Wsel_v': 8.0,
     'L0_ffn_Wsel_o': 8.0}
    for name, (base, spread) in spreads.items():
        noise = np.random.default_rng([zlib.crc32(name.encode()), seed]).standard_normal(out[name].shape)
        drawn = base * np.exp(spread * noise) if base else spread * noise
        out[name] = jnp.asarray(drawn.astype(out[name].dtype))
    for name, factor in factors.items():
        out[name] = (out[name] * factor).astype(out[name].dtype)
    return out
```

```python
from contextlib import ExitStack

import concourse.bass as bass
from concourse import mybir

B, S, D = 8, 512, 256
H = 16
CA = D // H
P, E = 64, 8
F = 1024
NROT = 32
HALF = NROT // 2
EPS = 1e-5
NP = 128
TT = S // NP
KC = D // NP
FC = F // NP
HP = H // 2
NQK = 4 * P
NA = 6 * CA
NPROJ = NQK + NA
EP = E // 2
G2 = 2 * E
STK = 6 * CA
BIG = 1e30
SIG_ONE = 17.4

J_PROJ, J_V0, J_QT, J_KT, J_SQ, J_SK, J_V1 = 0, 4, 8, 9, 10, 11, 12
J_GT = (16, 23)
J_PVB = (17, 24)
J_PVA = (18, 25)
J_G = (19, 26)
NJ = 30
UNITS = 16
X_T, X_GATE, X_S1T, X_F1, X_F2, X_WO, NX = 0, 2, 6, 8, 16, 20, 24
XB = 4
PRIME = 2


def unit(u):
    return u // 8, (u % 8) // 2, u % 2 == 1


def build(nc, x, wqk, wv, wo, wsel, w_out, w1, w2, b1, rows, ident, ident_h, mask, sel, rope, rank, a_scratch, out):
    f32, bf16 = mybir.dt.float32, mybir.dt.bfloat16
    ALU, ACT, AX = mybir.AluOpType, mybir.ActivationFunctionType, mybir.AxisListType
    x_v = x.rearrange("b (t p) d -> b p t d", p=NP)
    out_v = out.rearrange("b (t p) d -> b p t d", p=NP)
    with ExitStack() as ctx:
        def sb(name, shape, dt=f32):
            return ctx.enter_context(nc.sbuf_tensor(name, shape, dt))

        def sem(name):
            return ctx.enter_context(nc.semaphore(name))

        first_dve = sb("first_dve", [1, 8])
        first_act = sb("first_act", [1, 8])
        ident_sb = sb("ident_sb", [NP, NP])
        ident_hb = sb("ident_hb", [NP, NP], bf16)
        mask_sb = sb("mask_sb", [NP, NP], bf16)
        sel_sb = sb("sel_sb", [NP, EP, NP], bf16)
        rope_sb = sb("rope_sb", [NP, 2, TT, HALF])
        rank_sb = sb("rank_sb", [NP, E])
        rows_sb = sb("rows_sb", [NP, 5, D])
        b1_sb = sb("b1_sb", [NP, FC])
        wsel_sb = sb("wsel_sb", [NP, KC, 2 * H * E])
        w_out_sb = sb("w_out_sb", [NP, KC, D])
        w1_sb = sb("w1_sb", [NP, KC, F])
        w2_sb = sb("w2_sb", [NP, FC, D])
        zero_hb = sb("zero_hb", [NP, S], bf16)
        wqk_sb = sb("wqk_sb", [NP, KC, NPROJ])
        wv_sb = sb("wv_sb", [NP, KC, 2 * E * P])
        wo_sb = sb("wo_sb", [NP, 2 * EP, D])
        x_sb = sb("x_sb", [NP, TT, D])
        xn = sb("xn", [NP, TT, D])
        xnT = sb("xnT", [NP, KC, S])
        stats = sb("stats", [NP, TT, 6])
        mv = sb("mv", [NP, TT, 2])
        var = sb("var", [NP, TT])
        root = sb("root", [NP, TT])
        rstd = sb("rstd", [NP, TT])
        logit = sb("logit", [NP, TT, 2 * H * E])
        sig = sb("sig", [NP, TT, 2 * H * E])
        gate = sb("gate", [NP, TT, 2 * H * E])
        pick = sb("pick", [NP, TT, 2 * H * E])
        best = sb("best", [NP, TT, 2 * H])
        s1 = sb("s1", [NP, TT, D])
        s1T = sb("s1T", [NP, KC, S])
        hT = sb("hT", [NP, FC, S])
        aT = sb("aT", [NP, KC, S])
        acc = sb("acc", [NP, TT, D])
        fin = sb("fin", [NP, TT, D])
        raw = sb("raw", [NP, TT, NPROJ])
        rot = sb("rot", [NP, 4, TT, 4, HALF])
        qT = sb("qT", [NP, S])
        kz = sb("kz", [NP, 2, S])
        part = sb("part", [NP, 4, TT, 3, CA], bf16)
        rest = sb("rest", [NP, 2, 4, TT, CA])
        stack = sb("stack", [NP, 4, TT, 6, CA], bf16)
        stackT = sb("stackT", [STK, 4, S], bf16)
        gates = sb("gates", [NP, TT, 2, G2])
        vm = sb("vm", [NP, 2, E * P])
        v_sb = sb("v_sb", [NP, TT, 2, P])
        peak = sb("peak", [NP, UNITS])
        bias = sb("bias", [NP, UNITS])
        den = sb("den", [NP, 2, 2, TT])
        rden = sb("rden", [NP, 2, 2, TT])
        probs = sb("probs", [NP, 2, S])
        ptb = sb("ptb", [NP, TT, S])
        pta = sb("pta", [NP, TT, S])
        gs = sb("gs", [NP, 2, 3, TT, E])
        gpart = sb("gpart", [NP, 2, TT, 3, E], bf16)
        gT = sb("gT", [NP, S], bf16)
        oT = sb("oT", [NP, S])
        u_sb = sb("u_sb", [NP, 2, S])
        a_st = sb("a_st", [CA, 2, S])

        bank = [ctx.enter_context(nc.psum_tensor(f"bank{i}", [NP, S], f32)) for i in range(8)]
        ybank = [bank[0], bank[1]]
        sbank = [bank[2], bank[3]]
        tbank = [bank[4], bank[5]]
        wbank = [bank[6], bank[7]]
        xbank = bank[2:6]

        consts_in = sem("consts_in")
        x_in = sem("x_in")
        wqk_in, wv_in, wo_in = sem("wqk_in"), sem("wv_in"), sem("wo_in")
        a_stored = [sem("a_stored0"), sem("a_stored1")]
        a_in = sem("a_in")
        out_stored = sem("out_stored")
        zeroed = sem("zeroed")
        x_full = sem("x_full")
        x_free = [sem(f"x_free{i}") for i in range(XB)]
        xn_ready = sem("xn_ready")
        var_ready = sem("var_ready")
        root_ready = sem("root_ready")
        sig_ready = sem("sig_ready")
        y_free = sem("y_free")
        s1_ready = sem("s1_ready")
        batch_done = sem("batch_done")
        w_full = sem("w_full")
        w_free = [sem("w_free0"), sem("w_free1")]
        rope_ready = sem("rope_ready")
        stack_ready = sem("stack_ready")
        v_ready = sem("v_ready")
        s_full = sem("s_full")
        bias_ready = sem("bias_ready")
        exp_done = sem("exp_done")
        a_scaled = sem("a_scaled")
        t_full = sem("t_full")
        t_free = sem("t_free")
        gpart_ready = sem("gpart_ready")
        o_done = sem("o_done")
        dve_step = sem("dve_step")
        batch_step = sem("batch_step")
        pool_step = sem("pool_step")

        block = ctx.enter_context(nc.Block())

        @block.sync
        def _(sp):
            for dst, src in ((ident_sb[:], ident), (ident_hb[:], ident_h), (mask_sb[:], mask), (sel_sb[:], sel),
                             (rope_sb[:], rope), (rank_sb[:], rank), (b1_sb[:], b1), (rows_sb[:], rows),
                             (wsel_sb[:], wsel), (w_out_sb[:], w_out), (w1_sb[:], w1), (w2_sb[:], w2)):
                sp.dma_start(dst, src).then_inc(consts_in, 16)
            with sp.Fori(0, B) as b:
                sp.wait_ge(batch_done, b + PRIME)
                sp.wait_ge(out_stored, b * 16 + PRIME)
                sp.dma_start(x_sb[:], x_v[bass.ds(b, 1), :, :, :].rearrange("b p t d -> p (b t) d")).then_inc(x_in, 16)
                with sp.Fori(0, HP) as p:
                    it = b * HP + p
                    sp.wait_ge(rope_ready, it + PRIME)
                    sp.dma_start(wqk_sb[:], wqk[bass.ds(p, 1), :, :, :].rearrange("o q k n -> (o q) k n")).then_inc(wqk_in, 16)
                    sp.wait_ge(v_ready, it * 2 * TT + PRIME)
                    sp.dma_start(wv_sb[:], wv[bass.ds(p, 1), :, :, :].rearrange("o q k n -> (o q) k n")).then_inc(wv_in, 16)
                    sp.wait_ge(o_done, it * 2 * EP + PRIME)
                    sp.dma_start(wo_sb[:], wo[bass.ds(p, 1), :, :, :].rearrange("o q k n -> (o q) k n")).then_inc(wo_in, 16)
                for j in range(2):
                    sp.wait_ge(a_stored[j], b * (HP * 16) + HP * 16)
                sp.dma_start(aT[:], a_scratch.rearrange("(k q) t -> q k t", q=NP)).then_inc(a_in, 16)
                sp.wait_ge(batch_done, b + 1 + PRIME)
                sp.dma_start(out_v[bass.ds(b, 1), :, :, :].rearrange("b p t d -> p (b t) d"), fin[:]).then_inc(out_stored, 16)


            sp.wait_ge(out_stored, B * 16 + PRIME)

        @block.gpsimd
        def _(pool):
            nc.gpsimd.memset(zero_hb[:], 0.0).then_inc(zeroed, 1)
            nc.gpsimd.memset(kz[:], 0.0).then_inc(zeroed, 1)
            nc.gpsimd.memset(gT[:], 0.0).then_inc(zeroed, 1)
            with pool.Fori(0, B) as b:
                with pool.Fori(0, HP) as p:
                    it = b * HP + p
                    n = 0
                    STEPS = 4

                    def made(ins):
                        nonlocal n
                        n += 1
                        ins.then_inc(pool_step, 1)
                        pool.wait_ge(pool_step, it * STEPS + n)

                    pool.wait_ge(w_free[0], it * (NJ // 2) + 2 + PRIME)
                    pool.wait_ge(w_free[1], it * (NJ // 2) + 2 + PRIME)
                    src = raw[:, :, NQK:NQK + 4 * CA].rearrange("q t (g c) -> q g t c", g=4)
                    zeros = zero_hb[:, 0:4 * TT * CA].rearrange("q (g t c) -> q g t c", g=4, t=TT)
                    made(nc.gpsimd.tensor_tensor(part[:, :, :, 0, :], src, zeros, ALU.add))
                    made(nc.gpsimd.tensor_tensor(rest[:, 0], src, part[:, :, :, 0, :], ALU.subtract))
                    made(nc.gpsimd.tensor_tensor(part[:, :, :, 1, :], rest[:, 0], zeros, ALU.add))
                    made(nc.gpsimd.tensor_tensor(part[:, :, :, 2, :], rest[:, 0], part[:, :, :, 1, :], ALU.subtract))
                    pq = part[:, 0:2].rearrange("q g t s c -> q (g t) s c")
                    pk = part[:, 2:4].rearrange("q g t s c -> q (g t) s c")
                    sq = stack[:, 0:2].rearrange("q g t s c -> q (g t) s c")
                    sk = stack[:, 2:4].rearrange("q g t s c -> q (g t) s c")
                    nc.gpsimd.tensor_tensor(sq[:, :, 0:3, :], pq[:, :, 0:1, :].to_broadcast([NP, 2 * TT, 3, CA]),
                                            zero_hb[:, 0:6 * TT * CA].rearrange("q (g s c) -> q g s c", s=3, c=CA), ALU.add).then_inc(stack_ready, 1)
                    nc.gpsimd.tensor_copy(sq[:, :, 3:5, :], pq[:, :, 1:2, :].to_broadcast([NP, 2 * TT, 2, CA])).then_inc(stack_ready, 1)
                    nc.gpsimd.tensor_copy(sq[:, :, 5, :], pq[:, :, 2, :]).then_inc(stack_ready, 1)
                    nc.gpsimd.tensor_copy(sk[:, :, 0:3, :], pk).then_inc(stack_ready, 1)
                    nc.gpsimd.tensor_copy(sk[:, :, 3:5, :], pk[:, :, 0:2, :]).then_inc(stack_ready, 1)
                    nc.gpsimd.tensor_copy(sk[:, :, 5, :], pk[:, :, 0, :]).then_inc(stack_ready, 1)
                    for j in range(2):
                        pool.wait_ge(w_free[J_PVA[j] % 2], it * (NJ // 2) + J_PVA[j] // 2 + 1 + PRIME)
                        row = p * (2 * CA) + j * CA
                        if j == 0:
                            pool.wait_ge(batch_done, b + PRIME)
                        pool.dma_start(a_scratch[bass.ds(row, CA), :], a_st[:, j, :]).then_inc(a_stored[j], 16)
                    for j in range(2):
                        pool.wait_ge(a_stored[j], it * 16 + 16)

        @block.tensor
        def _(pe):
            pe.wait_ge(consts_in, 12 * 16)
            pe.wait_ge(zeroed, 3)
            for i, s in enumerate((w_full, o_done, t_full)):
                nc.tensor.matmul(bank[7][:, 16 * i:16 * i + 16], zero_hb[:, 0:NP], zero_hb[:, 0:16], start=True, stop=True).then_inc(s, PRIME)

            with pe.Fori(0, B) as b:
                def x_bank(n):
                    pe.wait_ge(x_free[n % XB], b * (NX // XB) + n // XB + PRIME)
                    return xbank[n % XB]

                def x_read(n):
                    pe.wait_ge(x_free[n % XB], b * (NX // XB) + n // XB + 1 + PRIME)

                pe.wait_ge(xn_ready, b + 1)
                for k in range(KC):
                    o = x_bank(X_T + k)
                    for t in range(TT):
                        mm = nc.tensor.transpose(o[:, t * NP:(t + 1) * NP], xn[:, t, k * NP:(k + 1) * NP], ident_sb[:])
                    mm.then_inc(x_full, 1)
                x_read(X_T)
                x_read(X_T + 1)
                for t in range(TT):
                    o = x_bank(X_GATE + t)
                    for k in range(KC):
                        mm = nc.tensor.matmul(o[:, 0:2 * H * E], xnT[:, k, t * NP:(t + 1) * NP], wsel_sb[:, k, :], start=k == 0, stop=k == KC - 1)
                    mm.then_inc(x_full, 1)
                for n in range(X_GATE, X_S1T):
                    x_read(n)
                pe.wait_ge(y_free, b * 2 + PRIME)
                for y in ybank:
                    nc.tensor.matmul(y[:], zero_hb[:, 0:NP], zero_hb[:], start=True, stop=True, skip_group_check=True)

                with pe.Fori(0, HP) as p:
                    it = b * HP + p

                    def w_bank(n):
                        pe.wait_ge(w_free[n % 2], it * (NJ // 2) + n // 2 + PRIME)
                        return wbank[n % 2]

                    def v_job(j, t, n):
                        o = w_bank(n)
                        for k in range(KC):
                            mm = nc.tensor.matmul(o[:], xnT[:, k, t * NP:(t + 1) * NP], wv_sb[:, k, j * E * P:(j + 1) * E * P], start=k == 0, stop=k == KC - 1)
                        mm.then_inc(w_full, 1)

                    def scores(u):
                        j, qt, causal = unit(u)
                        pe.wait_ge(exp_done, it * UNITS + u - 1 + PRIME)
                        o = sbank[u % 2]
                        qs = slice(qt * NP, (qt + 1) * NP)
                        if causal:
                            nc.tensor.matmul(o[:, 0:(qt + 1) * NP], stackT[:, j, qs], stackT[:, 2 + j, 0:(qt + 1) * NP], start=True, stop=False)
                            mm = nc.tensor.matmul(o[:, qs], ident_hb[:], mask_sb[:], start=False, stop=True)
                        else:
                            mm = nc.tensor.matmul(o[:], qT[:, qs], kz[:, j, :], start=True, stop=True)
                        mm.then_inc(s_full, 1)

                    def turn(u):
                        j, qt, causal = unit(u)
                        pe.wait_ge(t_free, it * UNITS + u - 1 + PRIME)
                        if causal:
                            pe.wait_ge(a_scaled, it * 8 + u // 2 + 1)
                        else:
                            pe.wait_ge(exp_done, it * UNITS + u + 1 + PRIME)
                        for c in range(qt + 1 if causal else TT):
                            mm = nc.tensor.transpose(tbank[u % 2][:, c * NP:(c + 1) * NP], probs[:, u % 2, c * NP:(c + 1) * NP], ident_sb[:])
                        mm.then_inc(t_full, 1)

                    def attend(j):
                        o = w_bank(J_GT[j])
                        pe.wait_ge(gpart_ready, it * 2 + j + 1)
                        for t in range(TT):
                            mm = nc.tensor.transpose(o.bitcast(bf16)[0:3 * E, t * NP:(t + 1) * NP], gpart[:, j, t].rearrange("q s e -> q (s e)"), ident_hb[:])
                        mm.then_inc(w_full, 1)
                        o = w_bank(J_PVB[j])
                        pe.wait_ge(v_ready, it * 2 * TT + TT * j + TT + PRIME)
                        pe.wait_ge(t_free, it * UNITS + 8 * j + 8 + PRIME)
                        for k in range(TT):
                            mm = nc.tensor.matmul(o[0:P, :], v_sb[:, k, j, :], ptb[:, k, :], start=k == 0, stop=k == TT - 1)
                        mm.then_inc(w_full, 1)
                        o = w_bank(J_PVA[j])
                        c0 = NQK + 4 * CA + j * CA
                        for k in range(TT):
                            mm = nc.tensor.matmul(o[0:CA, k * NP:S], raw[:, k, c0:c0 + CA], pta[:, k, k * NP:S], start=k == 0, stop=k == TT - 1)
                        mm.then_inc(w_full, 1)

                    def spread(j, e):
                        if e == 0:
                            pe.wait_ge(w_free[J_GT[j] % 2], it * (NJ // 2) + J_GT[j] // 2 + 1 + PRIME)
                        o = w_bank(J_G[j] + e)
                        nc.tensor.matmul(o[:], sel_sb[:, e, :], gT[:], start=True, stop=True).then_inc(w_full, 1)

                    def project(j, e):
                        n = j * EP + e
                        g = J_G[j] + e
                        pe.wait_ge(w_free[g % 2], it * (NJ // 2) + g // 2 + 1 + PRIME)
                        if n == 0:
                            pe.wait_ge(wo_in, it * 16 + 16)
                        for t in range(TT):
                            mm = nc.tensor.matmul(ybank[t // 2][:, (t % 2) * D:(t % 2 + 1) * D], u_sb[:, n % 2, t * NP:(t + 1) * NP], wo_sb[:, n, :], start=False, stop=False, skip_group_check=True)
                        mm.then_inc(o_done, 1)

                    pe.wait_ge(wqk_in, it * 16 + 16)
                    for t in range(TT):
                        o = w_bank(J_PROJ + t)
                        for k in range(KC):
                            mm = nc.tensor.matmul(o[:, 0:NPROJ], xnT[:, k, t * NP:(t + 1) * NP], wqk_sb[:, k, :], start=k == 0, stop=k == KC - 1)
                        mm.then_inc(w_full, 1)
                    pe.wait_ge(wv_in, it * 16 + 16)
                    for t in range(TT):
                        v_job(0, t, J_V0 + t)
                    pe.wait_ge(rope_ready, it + 1 + PRIME)
                    for n in (J_QT, J_KT):
                        o = w_bank(n)
                        c0 = (n - J_QT) * 2 * P
                        for t in range(TT):
                            mm = nc.tensor.transpose(o[:, t * NP:(t + 1) * NP], raw[:, t, c0:c0 + 2 * P], ident_sb[:])
                        mm.then_inc(w_full, 1)
                    pe.wait_ge(stack_ready, it * 6 + 6)
                    for n in (J_SQ, J_SK):
                        o = w_bank(n)
                        for g in range(2):
                            for t in range(TT):
                                mm = nc.tensor.transpose(o.bitcast(bf16)[0:STK, (g * TT + t) * NP:(g * TT + t + 1) * NP],
                                                         stack[:, 2 * (n - J_SQ) + g, t].rearrange("q s c -> q (s c)"), ident_hb[:])
                        mm.then_inc(w_full, 1)
                    pe.wait_ge(w_free[0], it * (NJ // 2) + J_SQ // 2 + 1 + PRIME)
                    pe.wait_ge(w_free[1], it * (NJ // 2) + J_SK // 2 + 1 + PRIME)
                    scores(0)
                    for u in range(UNITS):
                        if u + 1 < UNITS:
                            scores(u + 1)
                        if u < TT:
                            v_job(1, u, J_V1 + u)
                        elif u == 8:
                            attend(0)
                        elif u == 9:
                            spread(0, 0)
                            spread(0, 1)
                            project(0, 0)
                        elif u in (10, 11):
                            spread(0, u - 8)
                            project(0, u - 9)
                        elif u == 12:
                            project(0, 3)
                        turn(u)
                    attend(1)
                    spread(1, 0)
                    spread(1, 1)
                    project(1, 0)
                    spread(1, 2)
                    project(1, 1)
                    spread(1, 3)
                    project(1, 2)
                    project(1, 3)

                pe.wait_ge(exp_done, b * (HP * UNITS) + HP * UNITS + PRIME)
                pe.wait_ge(t_free, b * (HP * UNITS) + HP * UNITS + PRIME)
                pe.wait_ge(s1_ready, b + 1)
                for k in range(KC):
                    o = x_bank(X_S1T + k)
                    for t in range(TT):
                        mm = nc.tensor.transpose(o[:, t * NP:(t + 1) * NP], s1[:, t, k * NP:(k + 1) * NP], ident_sb[:])
                    mm.then_inc(x_full, 1)
                x_read(X_S1T)
                x_read(X_S1T + 1)
                for f in range(FC):
                    o = x_bank(X_F1 + f)
                    for k in range(KC):
                        mm = nc.tensor.matmul(o[:], w1_sb[:, k, f * NP:(f + 1) * NP], s1T[:, k, :], start=k == 0, stop=k == KC - 1)
                    mm.then_inc(x_full, 1)
                for n in range(X_F2 - XB, X_F2):
                    x_read(n)
                for t in range(TT):
                    o = x_bank(X_F2 + t)
                    for f in range(FC):
                        mm = nc.tensor.matmul(o[:, 0:D], hT[:, f, t * NP:(t + 1) * NP], w2_sb[:, f, :], start=f == 0, stop=f == FC - 1)
                    mm.then_inc(x_full, 1)
                pe.wait_ge(a_in, b * 16 + 16)
                for t in range(TT):
                    o = x_bank(X_WO + t)
                    for k in range(KC):
                        mm = nc.tensor.matmul(o[:, 0:D], aT[:, k, t * NP:(t + 1) * NP], w_out_sb[:, k, :], start=k == 0, stop=k == KC - 1)
                    mm.then_inc(x_full, 1)

        @block.scalar
        def _(act):
            act.wait_ge(consts_in, 12 * 16)
            for i, s in enumerate((exp_done, t_free, *x_free, *w_free)):
                nc.scalar.activation(first_act[:, i:i + 1], ident_sb[0:1, 0:1], ACT.Copy).then_inc(s, PRIME)
            with act.Fori(0, B) as b:
                def roots(i):
                    act.wait_ge(var_ready, b * 3 + i + 1)
                    nc.scalar.activation(root[:], var[:], ACT.Sqrt).then_inc(root_ready, 1)

                roots(0)
                for k in range(KC):
                    act.wait_ge(x_full, b * NX + X_T + k + 1)
                    nc.scalar.activation(xnT[:, k, :], xbank[(X_T + k) % XB][:], ACT.Copy).then_inc(x_free[(X_T + k) % XB], 1)
                for t in range(TT):
                    act.wait_ge(x_full, b * NX + X_GATE + t + 1)
                    nc.scalar.activation(logit[:, t, :], xbank[(X_GATE + t) % XB][:, 0:2 * H * E], ACT.Copy).then_inc(x_free[(X_GATE + t) % XB], 1)
                for n in range(X_GATE, X_S1T):
                    act.wait_ge(x_free[n % XB], b * (NX // XB) + n // XB + 1 + PRIME)
                nc.scalar.activation(sig[:], logit[:], ACT.Sigmoid).then_inc(sig_ready, 1)
                with act.Fori(0, HP) as p:
                    it = b * HP + p

                    def drain(n, dst, src):
                        act.wait_ge(w_full, it * NJ + n + 1 + PRIME)
                        return nc.scalar.activation(dst, src, ACT.Copy)

                    def exps(u):
                        j, qt, causal = unit(u)
                        w = (qt + 1) * NP if causal else S
                        act.wait_ge(bias_ready, it * UNITS + u + 1)
                        act.wait_ge(t_full, it * UNITS + u - 1 + PRIME)
                        nc.scalar.activation(probs[:, u % 2, 0:w], sbank[u % 2][:, 0:w], ACT.Exp, bias=bias[:, u:u + 1],
                                             scale=CA ** -0.5 if causal else P ** -0.5,
                                             accum_out=den[:, j, int(causal), qt:qt + 1]).then_inc(exp_done, 1)

                    def turned(u):
                        j, qt, causal = unit(u)
                        act.wait_ge(t_full, it * UNITS + u + 1 + PRIME)
                        n = qt + 1 if causal else TT
                        dst = pta if causal else ptb
                        nc.scalar.activation(dst[:, 0:n, qt * NP:(qt + 1) * NP], tbank[u % 2][:, 0:n * NP].rearrange("q (c m) -> q c m", m=NP),
                                             ACT.Copy).then_inc(t_free, 1)

                    for t in range(TT):
                        drain(J_PROJ + t, raw[:, t, :], wbank[t % 2][:, 0:NPROJ]).then_inc(w_free[t % 2], 1)
                    drain(J_QT, qT[:], wbank[0][:]).then_inc(w_free[0], 1)
                    act.wait_ge(w_full, it * NJ + J_KT + 1 + PRIME)
                    nc.scalar.activation(kz[0:P, 0, :], wbank[1][0:P, :], ACT.Copy)
                    nc.scalar.activation(kz[P:NP, 1, :], wbank[1][P:NP, :], ACT.Copy).then_inc(w_free[1], 1)
                    for n in (J_SQ, J_SK):
                        g = 2 * (n - J_SQ)
                        drain(n, stackT[:, g:g + 2, :], wbank[n % 2].bitcast(bf16)[0:STK, :].rearrange("q (g s) -> q g s", g=2)).then_inc(w_free[n % 2], 1)
                    exps(0)

                    def attend(j):
                        drain(J_GT[j], gT[0:3 * E, :], wbank[J_GT[j] % 2].bitcast(bf16)[0:3 * E, 0:S]).then_inc(w_free[J_GT[j] % 2], 1)
                        drain(J_PVB[j], oT[0:P, :], wbank[J_PVB[j] % 2][0:P, :])
                        nc.scalar.activation(oT[P:NP, :], wbank[J_PVB[j] % 2][0:P, :], ACT.Copy).then_inc(w_free[J_PVB[j] % 2], 1)
                        drain(J_PVA[j], a_st[:, j, :], wbank[J_PVA[j] % 2][0:CA, :]).then_inc(w_free[J_PVA[j] % 2], 1)

                    for u in range(UNITS):
                        if u + 1 < UNITS:
                            exps(u + 1)
                        if u == 8:
                            attend(0)
                        turned(u)
                    attend(1)
                roots(1)
                for k in range(KC):
                    act.wait_ge(x_full, b * NX + X_S1T + k + 1)
                    nc.scalar.activation(s1T[:, k, :], xbank[(X_S1T + k) % XB][:], ACT.Copy).then_inc(x_free[(X_S1T + k) % XB], 1)
                for f in range(FC):
                    act.wait_ge(x_full, b * NX + X_F1 + f + 1)
                    nc.scalar.activation(hT[:, f, :], xbank[(X_F1 + f) % XB][:], ACT.Relu, bias=b1_sb[:, f:f + 1]).then_inc(x_free[(X_F1 + f) % XB], 1)
                roots(2)

        @block.vector
        def _(dve):
            BSTEPS, PSTEPS = 41, 36
            dve.wait_ge(consts_in, 12 * 16)
            dve.wait_ge(zeroed, 3)
            for i, s in enumerate((v_ready, rope_ready, y_free, batch_done, out_stored)):
                nc.vector.memset(first_dve[:, i:i + 1], 0.0).then_inc(s, PRIME)
            with dve.Fori(0, B) as b:
                nb = 0

                def made(ins):
                    nonlocal nb
                    nb += 1
                    ins.then_inc(batch_step, 1)
                    dve.wait_ge(batch_step, b * BSTEPS + nb)

                def normalize(dst, src, i):
                    for t in range(TT):
                        last = nc.vector.bn_stats(stats[:, t, :], src[:, t, :])
                    made(last)
                    nc.vector.memset(var[:], 0.0)
                    for t in range(TT):
                        last = nc.vector.bn_aggr(mv[:, t, :], stats[:, t, :])
                    made(last)
                    nc.vector.tensor_scalar(var[:], mv[:, :, 1], EPS, None, ALU.add).then_inc(var_ready, 1)
                    dve.wait_ge(root_ready, b * 3 + i + 1)
                    made(nc.vector.reciprocal(rstd[:], root[:]))
                    made(nc.vector.tensor_tensor(root[:], var[:], rstd[:], ALU.mult))
                    made(nc.vector.tensor_tensor(root[:], root[:], rstd[:], ALU.mult))
                    made(nc.vector.tensor_scalar(root[:], root[:], -0.5, 1.5, ALU.mult, ALU.add))
                    made(nc.vector.tensor_tensor(rstd[:], rstd[:], root[:], ALU.mult))
                    for t in range(TT):
                        last = nc.vector.tensor_scalar(dst[:, t, :], src[:, t, :], mv[:, t, 0:1], rstd[:, t:t + 1], ALU.subtract, ALU.mult)
                    return last

                def row(i):
                    return rows_sb[:, i:i + 1, :].to_broadcast([NP, TT, D])

                dve.wait_ge(x_in, b * 16 + 16)
                normalize(xn, x_sb, 0).then_inc(xn_ready, 1)
                for n in range(X_GATE, X_S1T):
                    dve.wait_ge(x_free[n % XB], b * (NX // XB) + n // XB + 1 + PRIME)
                level = gate[:].rearrange("q t (g e) -> q (t g) e", e=E)
                one = pick[:].rearrange("q t (g e) -> q (t g) e", e=E)
                two = fin[:].rearrange("q t (g e) -> q (t g) e", e=E)
                top = best[:].rearrange("q t g -> q (t g)")
                wide = [NP, TT * 2 * H, E]
                top_b = top.unsqueeze(2).to_broadcast(wide)
                rank_b = rank_sb[:, None, :].to_broadcast(wide)
                made(nc.vector.tensor_scalar(gate[:], logit[:], SIG_ONE, None, ALU.min))
                for dst in (one, two):
                    made(nc.vector.tensor_reduce(top, level, AX.X, ALU.max))
                    made(nc.vector.tensor_tensor(dst, level, top_b, ALU.is_equal))
                    made(nc.vector.tensor_tensor(dst, dst, rank_b, ALU.mult))
                    made(nc.vector.tensor_reduce(top, dst, AX.X, ALU.max))
                    made(nc.vector.tensor_tensor(dst, dst, top_b, ALU.is_equal))
                    if dst is one:
                        made(nc.vector.scalar_tensor_tensor(gate[:], pick[:], -BIG, gate[:], ALU.mult, ALU.add))
                made(nc.vector.tensor_tensor(pick[:], pick[:], fin[:], ALU.add))
                dve.wait_ge(sig_ready, b + 1)
                made(nc.vector.tensor_tensor(gate[:], sig[:], pick[:], ALU.mult))
                nc.vector.memset(peak[:], 0.0)

                with dve.Fori(0, HP) as p:
                    it = b * HP + p
                    n_p = 0

                    def step(ins):
                        nonlocal n_p
                        n_p += 1
                        ins.then_inc(dve_step, 1)
                        dve.wait_ge(dve_step, it * PSTEPS + n_p)

                    def v_gate(j, t, n):
                        dve.wait_ge(w_full, it * NJ + n + 1 + PRIME)
                        g = gates[:, t, 0, j * E:(j + 1) * E].unsqueeze(2).to_broadcast([NP, E, P])
                        i = n % 2
                        ins = nc.vector.tensor_tensor(vm[:, i, :].rearrange("q (e c) -> q e c", e=E), wbank[i][:].rearrange("q (e c) -> q e c", e=E), g, ALU.mult)
                        ins.then_inc(w_free[i], 1)
                        dve.wait_ge(w_free[i], it * (NJ // 2) + n // 2 + 1 + PRIME)
                        nc.vector.tensor_reduce(v_sb[:, t, j, :], vm[:, i, :].rearrange("q (e c) -> q c e", e=E), AX.X, ALU.add).then_inc(v_ready, 1)

                    def row_peak(u):
                        j, qt, causal = unit(u)
                        dve.wait_ge(s_full, it * UNITS + u + 1)
                        step(nc.vector.tensor_reduce(peak[:, u:u + 1], sbank[u % 2][:, 0:(qt + 1) * NP if causal else S], AX.X, ALU.max))
                        nc.vector.tensor_scalar(bias[:, u:u + 1], peak[:, u:u + 1], -(CA ** -0.5 if causal else P ** -0.5), None, ALU.mult).then_inc(bias_ready, 1)

                    def scale_probs(u):
                        j, qt, causal = unit(u)
                        w = (qt + 1) * NP
                        dve.wait_ge(exp_done, it * UNITS + u + 1 + PRIME)
                        step(nc.vector.reciprocal(rden[:, j, 1, qt:qt + 1], den[:, j, 1, qt:qt + 1]))
                        nc.vector.tensor_scalar(probs[:, u % 2, 0:w], probs[:, u % 2, 0:w], rden[:, j, 1, qt:qt + 1], None, ALU.mult).then_inc(a_scaled, 1)

                    def gate_parts(j):
                        dve.wait_ge(exp_done, it * UNITS + 8 * j + 7 + PRIME)
                        step(nc.vector.reciprocal(rden[:, j, 0, :], den[:, j, 0, :]))
                        step(nc.vector.tensor_tensor(gs[:, j, 0], gates[:, :, 1, j * E:(j + 1) * E], rden[:, j, 0, :].unsqueeze(2).to_broadcast([NP, TT, E]), ALU.mult))
                        step(nc.vector.tensor_copy(gpart[:, j, :, 0, :], gs[:, j, 0]))
                        step(nc.vector.tensor_tensor(gs[:, j, 1], gs[:, j, 0], gpart[:, j, :, 0, :], ALU.subtract))
                        step(nc.vector.tensor_copy(gpart[:, j, :, 1, :], gs[:, j, 1]))
                        nc.vector.tensor_tensor(gpart[:, j, :, 2, :], gs[:, j, 1], gpart[:, j, :, 1, :], ALU.subtract).then_inc(gpart_ready, 1)

                    def u_gate(j, e):
                        k = j * EP + e
                        n = J_G[j] + e
                        if e == 0:
                            dve.wait_ge(w_free[J_PVB[j] % 2], it * (NJ // 2) + J_PVB[j] // 2 + 1 + PRIME)
                        dve.wait_ge(w_full, it * NJ + n + 1 + PRIME)
                        dve.wait_ge(o_done, it * 2 * EP + k - 1 + PRIME)
                        nc.vector.tensor_tensor(u_sb[:, k % 2, :], wbank[n % 2][:], oT[:], ALU.mult).then_inc(w_free[n % 2], 1)

                    step(nc.vector.tensor_copy(gates[:], gate[:].rearrange("q t (v n) -> q t v n", v=2)[:, :, :, bass.ds(p * G2, G2)]))
                    for n in (J_PROJ + 2, J_PROJ + 3):
                        dve.wait_ge(w_free[n % 2], it * (NJ // 2) + n // 2 + 1 + PRIME)
                    head = raw[:, :, 0:NQK].rearrange("q t (g c) -> q t g c", g=4)
                    a, c = head[:, :, :, 0:HALF], head[:, :, :, HALF:NROT]
                    cos = rope_sb[:, 0].unsqueeze(2).to_broadcast([NP, TT, 4, HALF])
                    sin = rope_sb[:, 1].unsqueeze(2).to_broadcast([NP, TT, 4, HALF])
                    nc.vector.tensor_tensor(rot[:, 0], a, cos, ALU.mult)
                    nc.vector.tensor_tensor(rot[:, 1], c, sin, ALU.mult)
                    nc.vector.tensor_tensor(rot[:, 2], a, sin, ALU.mult)
                    step(nc.vector.tensor_tensor(rot[:, 3], c, cos, ALU.mult))
                    nc.vector.tensor_tensor(a, rot[:, 0], rot[:, 1], ALU.subtract)
                    nc.vector.tensor_tensor(c, rot[:, 2], rot[:, 3], ALU.add).then_inc(rope_ready, 1)
                    for t in range(TT):
                        v_gate(0, t, J_V0 + t)
                    row_peak(0)
                    for u in range(UNITS):
                        if u + 1 < UNITS:
                            row_peak(u + 1)
                        if unit(u)[2]:
                            scale_probs(u)
                        if u < TT:
                            v_gate(1, u, J_V1 + u)
                        if u % 8 == 7:
                            gate_parts(u // 8)
                        if u == 9:
                            u_gate(0, 0)
                            u_gate(0, 1)
                        if u in (10, 11):
                            u_gate(0, u - 8)
                    for e in range(EP):
                        u_gate(1, e)
                    assert n_p == PSTEPS, n_p

                dve.wait_ge(o_done, b * (HP * 2 * EP) + HP * 2 * EP + PRIME)
                for i, y in enumerate(ybank):
                    nc.vector.tensor_tensor(s1[:, 2 * i:2 * i + 2, :], y[:].rearrange("q (t d) -> q t d", t=2), xn[:, 2 * i:2 * i + 2, :], ALU.add).then_inc(y_free, 1)
                dve.wait_ge(y_free, b * 2 + 2 + PRIME)
                made(normalize(s1, s1, 1))
                made(nc.vector.tensor_tensor(s1[:], s1[:], row(0), ALU.mult))
                nc.vector.tensor_tensor(s1[:], s1[:], row(1), ALU.add).then_inc(s1_ready, 1)
                dve.wait_ge(s1_ready, b + 1)
                for t in range(TT):
                    dve.wait_ge(x_full, b * NX + X_F2 + t + 1)
                    nc.vector.tensor_tensor(acc[:, t, :], xbank[(X_F2 + t) % XB][:, 0:D], s1[:, t, :], ALU.add).then_inc(x_free[(X_F2 + t) % XB], 1)
                for t in range(TT):
                    dve.wait_ge(x_full, b * NX + X_WO + t + 1)
                    nc.vector.tensor_tensor(x_sb[:, t, :], xbank[(X_WO + t) % XB][:, 0:D], x_sb[:, t, :], ALU.add).then_inc(x_free[(X_WO + t) % XB], 1)
                for i in range(XB):
                    dve.wait_ge(x_free[i], b * (NX // XB) + NX // XB + PRIME)
                made(nc.vector.tensor_tensor(acc[:], acc[:], row(4), ALU.add))
                made(normalize(acc, acc, 2))
                made(nc.vector.tensor_tensor(acc[:], acc[:], row(2), ALU.mult))
                made(nc.vector.tensor_tensor(acc[:], acc[:], row(3), ALU.add))
                nc.vector.tensor_tensor(fin[:], acc[:], x_sb[:], ALU.add).then_inc(batch_done, 1)
                assert nb == BSTEPS, nb


def kernel(**inputs):
    import ml_dtypes
    import numpy as np
    import concourse.bacc as bacc
    from concourse import mybir as mb
    from concourse.bass_utils import run_bass_kernel_spmd

    a = {k: np.asarray(v) for k, v in inputs.items()}

    def chunks(w):
        return np.ascontiguousarray(w.reshape(-1, NP, w.shape[1]).transpose(1, 0, 2))

    f = "L0_ffn_"
    cols = []
    for h in range(0, H, 2):
        cols.append(np.concatenate(
            [a[f + "Wq"][h], a[f + "Wq"][h + 1], a[f + "Wk"][h], a[f + "Wk"][h + 1]]
            + [a["L0_attn_" + w][:, h * CA:(h + 2) * CA] for w in ("WQ", "WK", "WV")], axis=1))
    wqk = np.stack([chunks(c) for c in cols])
    wv = np.stack([chunks(a[f + "Wv"][h:h + 2].transpose(2, 0, 1, 3).reshape(D, 2 * E * P)) for h in range(0, H, 2)])
    wo = np.stack([chunks(a[f + "Wo"][h:h + 2].reshape(2 * E * P, D)) for h in range(0, H, 2)])
    wsel = chunks(np.concatenate([a[f + "Wsel_v"].reshape(H * E, D), a[f + "Wsel_o"].reshape(H * E, D)]).T)
    rows = np.stack([a[f + n] for n in ("ln1_g", "ln1_b", "ln2_g", "ln2_b", "b2")])
    rows = np.ascontiguousarray(np.broadcast_to(rows, (NP, 5, D)))
    inv = np.float32(10000.0) ** (-np.arange(HALF, dtype=np.float32) / np.float32(HALF))
    ang = np.arange(S, dtype=np.float32)[:, None] * inv[None, :]
    rope = np.stack([np.cos(ang), np.sin(ang)]).astype(np.float32).reshape(2, TT, NP, HALF).transpose(2, 0, 1, 3)
    bf = ml_dtypes.bfloat16
    mask = np.where(np.arange(NP)[None, :] > np.arange(NP)[:, None], -BIG, 0.0).astype(bf)
    sel = np.zeros((NP, EP, NP), bf)
    for s in range(3):
        for e in range(E):
            sel[s * E + e, e // 2, (e % 2) * P:(e % 2 + 1) * P] = 1
    rank = np.broadcast_to(np.arange(E, 0, -1, dtype=np.float32), (NP, E))
    arrays = {
        "x": a["L0_attn_x"], "wqk": wqk, "wv": wv, "wo": wo, "wsel": wsel, "w_out": chunks(a["L0_attn_WO"]),
        "w1": chunks(a[f + "W1"]), "w2": chunks(a[f + "W2"]), "b1": np.ascontiguousarray(a[f + "b1"].reshape(FC, NP).T),
        "rows": rows, "ident": np.eye(NP, dtype=np.float32), "ident_h": np.eye(NP).astype(bf), "mask": mask, "sel": sel,
        "rope": rope, "rank": rank,
    }
    arrays = {k: np.ascontiguousarray(v) for k, v in arrays.items()}
    nc = bacc.Bacc("TRN2", target_bir_lowering=False, num_devices=1)
    args = [nc.dram_tensor("in_" + k, v.shape, mb.dt.from_np(v.dtype), kind="ExternalInput").ap() for k, v in arrays.items()]
    scratch = nc.dram_tensor("a_scratch", (D, S), mb.dt.float32, kind="Internal").ap()
    out = nc.dram_tensor("out", (B, S, D), mb.dt.float32, kind="ExternalOutput").ap()
    build(nc, *args, scratch, out)
    r = run_bass_kernel_spmd(nc, [{"in_" + k: v for k, v in arrays.items()}], core_ids=[0])
    return r.results[0]["out"]
```

```python
from contextlib import ExitStack

import concourse.bass as bass
from concourse import mybir

B, S, D = 8, 512, 256
H = 16
CA = D // H
P, E = 64, 8
F = 1024
NROT = 32
HALF = NROT // 2
EPS = 1e-5
NP = 128
TT = S // NP
KC = D // NP
FC = F // NP
HP = H // 2
NQK = 4 * P
NA = 6 * CA
NPROJ = NQK + NA
EP = E // 2
G2 = 2 * E
STK = 6 * CA
BIG = 1e30
SIG_ONE = 17.4

UNITS = 16
HALF_U = 9
FILL = {9: [("pva", 0, 0), ("g", 0, 0), ("g", 0, 1)], 10: [("proj", 0, 0), ("proj", 0, 1)],
        11: [("o", 0, 0), ("proj", 0, 2)], 12: [("g", 0, 2), ("proj", 0, 3)], 13: [("o", 0, 1), ("g", 0, 3)],
        14: [("v", 1, 2), ("o", 0, 2)], 15: [("v", 1, 3), ("o", 0, 3)],
        0: [("v", 0, 1)], 1: [("v", 0, 2)], 2: [("g", 1, 2), ("o", 1, 1)], 3: [("g", 1, 3), ("o", 1, 2)],
        4: [("v", 0, 3)], 5: [("o", 1, 3)], 6: [("v", 1, 0)], 7: [("v", 1, 1)], 8: [("gt", 0, 0), ("pvb", 0, 0)]}
FRONT = [("gt", 1, 0), ("pvb", 1, 0), ("pva", 1, 0), ("g", 1, 0), ("g", 1, 1), ("v", 0, 0), ("o", 1, 0)]
FIRST, INNER, TAIL = range(3)


def of_last(job, u):
    if u is not None and u >= HALF_U:
        return job[0] != "proj"
    return job[0] in ("gt", "pvb", "pva", "g", "o") and job[1] == 1


ORDER = ([(j, of_last(j, u)) for u in range(HALF_U, UNITS) for j in FILL[u]] + [(j, of_last(j, None)) for j in FRONT]
         + [(j, of_last(j, u)) for u in range(HALF_U) for j in FILL[u]])
JOBS = [(j, last) for j, last in ORDER if j[0] != "o"]
NJ = len(JOBS)
LATE = [j for j, last in JOBS if last]
EARLY = [j for j, last in JOBS if not last]
X_T, X_GATE, X_S1T, X_F1, X_F2, X_WO, NX = 0, 2, 6, 8, 16, 20, 24
XB = 4
PRIME = 6


def unit(u):
    return u // 8, (u % 8) // 2, u % 2 == 1


def place(kind, job):
    if kind == FIRST:
        return EARLY.index(job)
    if kind == TAIL:
        return HP * NJ - len(LATE) + LATE.index(job)
    return [j for j, _ in JOBS].index(job) - len(LATE)


def place_done(kind, job):
    if job[1] == 1:
        return place(kind, job)
    return (HP * NJ if kind == TAIL else 0) + [j for j, _ in JOBS].index(job) - len(LATE) - NJ


def beside(kind, u):
    jobs = FRONT if u is None else FILL[u]
    return [j for j in jobs if kind == INNER or of_last(j, u) == (kind == TAIL)]


def build(nc, x, wqk, wv, wo, wsel, w_out, w1, w2, b1, rows, ident, ident_h, mask, sel, rope, rank, a_scratch, out):
    f32, bf16 = mybir.dt.float32, mybir.dt.bfloat16
    f32r = mybir.dt.float32r
    ALU, ACT, AX = mybir.AluOpType, mybir.ActivationFunctionType, mybir.AxisListType
    x_v = x.rearrange("b (t p) d -> b p t d", p=NP)
    out_v = out.rearrange("b (t p) d -> b p t d", p=NP)
    with ExitStack() as ctx:
        def sb(name, shape, dt=f32):
            return ctx.enter_context(nc.sbuf_tensor(name, shape, dt))

        def sem(name):
            return ctx.enter_context(nc.semaphore(name))

        first_dve = sb("first_dve", [1, 8])
        first_pool = sb("first_pool", [1, 8])
        primer = sb("primer", [1, 8])
        first_act = sb("first_act", [1, 16])
        ident_sb = sb("ident_sb", [NP, NP])
        ident_hb = sb("ident_hb", [NP, NP], bf16)
        mask_sb = sb("mask_sb", [NP, NP], bf16)
        sel_sb = sb("sel_sb", [NP, EP, NP], bf16)
        rope_sb = sb("rope_sb", [NP, 2, TT, HALF])
        rank_sb = sb("rank_sb", [NP, E])
        rows_sb = sb("rows_sb", [NP, 5, D])
        b1_sb = sb("b1_sb", [NP, FC])
        wsel_sb = sb("wsel_sb", [NP, KC, 2 * H * E])
        w_out_sb = sb("w_out_sb", [NP, KC, D])
        w1_sb = sb("w1_sb", [NP, KC, F])
        w2_sb = sb("w2_sb", [NP, FC, D])
        zero_hb = sb("zero_hb", [NP, S], bf16)
        wqk_sb = sb("wqk_sb", [NP, KC, NPROJ])
        wv_sb = sb("wv_sb", [NP, KC, 2 * E * P])
        wv_h = sb("wv_h", [NP, KC, 2 * E * P], f32r)
        wv_l = sb("wv_l", [NP, KC, 2 * E * P], f32r)
        wo_sb = sb("wo_sb", [NP, 2 * EP, D])
        x_sb = sb("x_sb", [NP, TT, D])
        xn = sb("xn", [NP, TT, D])
        xnT = sb("xnT", [NP, KC, S])
        xnT_h = sb("xnT_h", [NP, KC, S], f32r)
        xnT_l = sb("xnT_l", [NP, KC, S], f32r)
        stats = sb("stats", [NP, TT, 6])
        mv = sb("mv", [NP, TT, 2])
        var = sb("var", [NP, TT])
        root = sb("root", [NP, TT])
        rstd = sb("rstd", [NP, TT])
        logit = sb("logit", [NP, TT, 2 * H * E])
        sig = sb("sig", [NP, TT, 2 * H * E])
        gate = sb("gate", [NP, TT, 2 * H * E])
        pick = sb("pick", [NP, TT, 2 * H * E])
        best = sb("best", [NP, TT, 2 * H])
        s1 = logit
        s1T = sig[:].rearrange("q t n -> q (t n)").rearrange("q (k s) -> q k s", k=KC)
        aT = pick[:].rearrange("q t n -> q (t n)").rearrange("q (k s) -> q k s", k=KC)
        hT = sb("hT", [NP, FC, S])
        acc = sb("acc", [NP, TT, D])
        fin = sb("fin", [NP, TT, D])
        raw = sb("raw", [NP, TT, NPROJ])
        rot = sb("rot", [NP, 4, TT, 4, HALF])
        q_s = sb("q_s", [NP, 2, S], f32r)
        k_h = sb("k_h", [NP, 2, S], f32r)
        k_l = sb("k_l", [NP, 2, S], f32r)
        part = sb("part", [NP, 4, TT, 3, CA], bf16)
        rest = sb("rest", [NP, 2, 4, TT, CA])
        stack = sb("stack", [NP, 4, TT, 6, CA], bf16)
        stackT = sb("stackT", [STK, 4, S], bf16)
        gates = sb("gates", [NP, TT, 2, G2])
        vm = sb("vm", [NP, 2, E * P])
        v_sb = sb("v_sb", [NP, TT, 2, P])
        peak = sb("peak", [NP, UNITS])
        bias = sb("bias", [NP, UNITS])
        den = sb("den", [NP, 2, 2, TT])
        rden = sb("rden", [NP, 2, 2, TT])
        probs = sb("probs", [NP, 2, S])
        v_hl = sb("v_hl", [NP, TT, 2, 2 * P], f32r)
        ptb_h = sb("ptb_h", [NP, TT, S], f32r)
        ptb_l = sb("ptb_l", [NP, TT, S], f32r)
        o_low = sb("o_low", [P, S])
        pta = hT[:, 0:TT, :]
        gs = sb("gs", [NP, 2, 3, TT, E])
        gpart = sb("gpart", [NP, 2, TT, 3, E], bf16)
        gT = sb("gT", [NP, S], bf16)
        oT = sb("oT", [NP, S])
        u_sb = sb("u_sb", [NP, 2, S])
        va = sb("va", [NP, TT, 2 * CA])
        a_st = sb("a_st", [CA, 2, S])

        bank = [ctx.enter_context(nc.psum_tensor(f"bank{i}", [NP, S], f32)) for i in range(8)]
        ybank = [bank[0], bank[1]]
        sbank = [bank[2], bank[3]]
        tbank = [bank[4], bank[5]]
        wbank = [bank[6], bank[7]]
        xbank = bank[2:6]

        consts_in = sem("consts_in")
        x_in = sem("x_in")
        wqk_in = sem("wqk_in")
        wv_in = [sem("wv_in0"), sem("wv_in1")]
        wo_in = [sem("wo_in0"), sem("wo_in1")]
        a_stored = [sem("a_stored0"), sem("a_stored1")]
        a_in = sem("a_in")
        out_stored = sem("out_stored")
        zeroed = sem("zeroed")
        x_full = sem("x_full")
        x_free = [sem(f"x_free{i}") for i in range(XB)]
        xn_ready = sem("xn_ready")
        var_ready = sem("var_ready")
        root_ready = sem("root_ready")
        sig_ready = sem("sig_ready")
        y_free = sem("y_free")
        s1_ready = sem("s1_ready")
        batch_done = sem("batch_done")
        w_full = sem("w_full")
        w_free = [sem("w_free0"), sem("w_free1")]
        rope_ready = sem("rope_ready")
        va_ready = sem("va_ready")
        stack_ready = sem("stack_ready")
        v_ready = sem("v_ready")
        s_full = sem("s_full")
        bias_ready = sem("bias_ready")
        exp_done = sem("exp_done")
        a_scaled = sem("a_scaled")
        t_full = sem("t_full")
        t_free = [sem("t_free_expert"), sem("t_free_causal")]
        t_high = sem("t_high")
        o_half = sem("o_half")
        qk_full, qk_high, qk_low = sem("qk_full"), sem("qk_high"), sem("qk_low")
        stack_full, stack_out = sem("stack_full"), sem("stack_out")
        wv_split = [sem("wv_split0"), sem("wv_split1")]
        xnT_high = sem("xnT_high")
        xnT_split = sem("xnT_split")
        v_split = sem("v_split")
        gpart_ready = sem("gpart_ready")
        o_done = sem("o_done")
        dve_step = sem("dve_step")
        batch_step = sem("batch_step")
        pool_step = sem("pool_step")

        block = ctx.enter_context(nc.Block())

        @block.sync
        def _(sp):
            for dst, src in ((ident_sb[:], ident), (ident_hb[:], ident_h), (mask_sb[:], mask), (sel_sb[:], sel),
                             (rope_sb[:], rope), (rank_sb[:], rank), (b1_sb[:], b1), (rows_sb[:], rows),
                             (wsel_sb[:], wsel), (w_out_sb[:], w_out), (w1_sb[:], w1), (w2_sb[:], w2)):
                sp.dma_start(dst, src).then_inc(consts_in, 16)
            with sp.Fori(0, B) as b:
                sp.wait_ge(batch_done, b + PRIME)
                sp.wait_ge(out_stored, b * 16 + PRIME)
                sp.dma_start(x_sb[:], x_v[bass.ds(b, 1), :, :, :].rearrange("b p t d -> p (b t) d")).then_inc(x_in, 16)
                with sp.Fori(0, HP) as p:
                    it = b * HP + p
                    sp.wait_ge(rope_ready, it + PRIME)
                    sp.dma_start(wqk_sb[:], wqk[bass.ds(p, 1), :, :, :].rearrange("o q k n -> (o q) k n")).then_inc(wqk_in, 16)
                    for j in range(2):
                        sp.wait_ge(wv_split[j], it + PRIME)
                        sp.dma_start(wv_sb[:, :, j * E * P:(j + 1) * E * P], wv[bass.ds(p, 1), :, :, j * E * P:(j + 1) * E * P].rearrange("o q k n -> (o q) k n")).then_inc(wv_in[j], 16)
                    for j in range(2):
                        sp.wait_ge(o_done, it * (2 * EP) + (j - 1) * EP + PRIME)
                        sp.dma_start(wo_sb[:, j * EP:(j + 1) * EP, :], wo[bass.ds(p, 1), :, j * EP:(j + 1) * EP, :].rearrange("o q k n -> (o q) k n")).then_inc(wo_in[j], 16)
                for j in range(2):
                    sp.wait_ge(a_stored[j], b * (HP * 16) + HP * 16 + PRIME)
                sp.dma_start(aT, a_scratch.rearrange("(k q) t -> q k t", q=NP)).then_inc(a_in, 16)
                sp.wait_ge(batch_done, b + 1 + PRIME)
                sp.dma_start(out_v[bass.ds(b, 1), :, :, :].rearrange("b p t d -> p (b t) d"), fin[:]).then_inc(out_stored, 16)


            sp.wait_ge(out_stored, B * 16 + PRIME)

        @block.gpsimd
        def _(pool):
            nc.gpsimd.memset(zero_hb[:], 0.0).then_inc(zeroed, 1)
            nc.gpsimd.memset(first_pool[:], 0.0).then_inc(zeroed, 1)
            for i, s in enumerate(wv_split):
                nc.gpsimd.memset(primer[:, i:i + 1], 0.0).then_inc(s, PRIME)
            nc.gpsimd.memset(gT[:], 0.0).then_inc(zeroed, 1)
            with pool.Fori(0, B) as b:
                def w_read(kind, b, p, job):
                    at = place(kind, job)
                    pool.wait_ge(w_free[at % 2], b * (HP * NJ // 2) + p * (NJ // 2) + at // 2 + 1 + PRIME)

                def pair(b, p, kind):
                    it = b * HP + p
                    last_it = it - 1 if kind == INNER else b * HP + (HP - 1)
                    n = 0
                    STEPS = 8

                    def made(ins):
                        nonlocal n
                        n += 1
                        ins.then_inc(pool_step, 1)
                        pool.wait_ge(pool_step, (last_it + 1 if kind != FIRST else it) * STEPS - (kind != FIRST) + n)

                    def split_wv(j):
                        cols = slice(j * E * P, (j + 1) * E * P)
                        pool.wait_ge(wv_in[j], it * 16 + 16)
                        pool.wait_ge(v_ready, it * (2 * TT) + (j - 1) * TT + PRIME)
                        made(nc.gpsimd.tensor_tensor(wv_h[:, :, cols], wv_sb[:, :, cols], zero_hb[:, None, :].to_broadcast([NP, KC, E * P]), ALU.add))
                        nc.gpsimd.tensor_tensor(wv_l[:, :, cols], wv_sb[:, :, cols], wv_h.bitcast(f32)[:, :, cols], ALU.subtract).then_inc(wv_split[j], 1)

                    def split_v(j, of):
                        pool.wait_ge(v_ready, of * (2 * TT) + TT * j + TT + PRIME)
                        made(nc.gpsimd.tensor_tensor(v_hl[:, :, j, 0:P], v_sb[:, :, j, :], zero_hb[:, 0:TT * P].rearrange("q (t c) -> q t c", t=TT), ALU.add))
                        nc.gpsimd.tensor_tensor(v_hl[:, :, j, P:2 * P], v_sb[:, :, j, :], v_hl.bitcast(f32)[:, :, j, 0:P], ALU.subtract).then_inc(v_split, 1)

                    if kind == TAIL:
                        split_v(1, last_it)
                        return
                    split_wv(0)
                    for t in (TT - 2, TT - 1):
                        w_read(kind, b, p, ("proj", 0, t))
                    src = raw[:, :, NQK:NQK + 4 * CA].rearrange("q t (g c) -> q g t c", g=4)
                    zeros = zero_hb[:, 0:4 * TT * CA].rearrange("q (g t c) -> q g t c", g=4, t=TT)
                    made(nc.gpsimd.tensor_tensor(part[:, :, :, 0, :], src, zeros, ALU.add))
                    made(nc.gpsimd.tensor_tensor(rest[:, 0], src, part[:, :, :, 0, :], ALU.subtract))
                    made(nc.gpsimd.tensor_tensor(part[:, :, :, 1, :], rest[:, 0], zeros, ALU.add))
                    made(nc.gpsimd.tensor_tensor(part[:, :, :, 2, :], rest[:, 0], part[:, :, :, 1, :], ALU.subtract))
                    pq = part[:, 0:2].rearrange("q g t s c -> q (g t) s c")
                    pk = part[:, 2:4].rearrange("q g t s c -> q (g t) s c")
                    sq = stack[:, 0:2].rearrange("q g t s c -> q (g t) s c")
                    sk = stack[:, 2:4].rearrange("q g t s c -> q (g t) s c")
                    nc.gpsimd.tensor_tensor(sq[:, :, 0:3, :], pq[:, :, 0:1, :].to_broadcast([NP, 2 * TT, 3, CA]),
                                            zero_hb[:, 0:6 * TT * CA].rearrange("q (g s c) -> q g s c", s=3, c=CA), ALU.add)
                    nc.gpsimd.tensor_copy(sq[:, :, 3:5, :], pq[:, :, 1:2, :].to_broadcast([NP, 2 * TT, 2, CA]))
                    nc.gpsimd.tensor_copy(sq[:, :, 5, :], pq[:, :, 2, :])
                    nc.gpsimd.tensor_copy(sk[:, :, 0:3, :], pk)
                    nc.gpsimd.tensor_copy(sk[:, :, 3:5, :], pk[:, :, 0:2, :])
                    nc.gpsimd.tensor_copy(sk[:, :, 5, :], pk[:, :, 0, :]).then_inc(stack_ready, 1)
                    if kind == INNER:
                        split_v(1, last_it)
                    split_wv(1)
                    if kind == INNER:
                        w_read(kind, b, p, ("pva", 1, 0))
                    nc.gpsimd.tensor_tensor(va[:], raw[:, :, NQK + 4 * CA:], zero_hb[:, 0:TT * 2 * CA].rearrange("q (t c) -> q t c", t=TT), ALU.add).then_inc(va_ready, 1)
                    split_v(0, it)
                    assert n == STEPS - (kind == FIRST), n

                for k in range(KC):
                    pool.wait_ge(x_free[(X_T + k) % XB], b * (NX // XB) + 1 + PRIME)
                    nc.gpsimd.tensor_tensor(xnT_h[:, k, :], xnT[:, k, :], zero_hb[:], ALU.add).then_inc(xnT_high, 1)
                    pool.wait_ge(xnT_high, b * KC + k + 1)
                    nc.gpsimd.tensor_tensor(xnT_l[:, k, :], xnT[:, k, :], xnT_h.bitcast(f32)[:, k, :], ALU.subtract).then_inc(xnT_split, 1)
                pair(b, 0, FIRST)
                with pool.Fori(1, HP) as p:
                    pair(b, p, INNER)
                pair(b, 0, TAIL)

        @block.tensor
        def _(pe):
            pe.wait_ge(consts_in, 12 * 16)
            pe.wait_ge(zeroed, 3)
            for i, s in enumerate((w_full, o_done, t_full)):
                nc.tensor.matmul(bank[7][:, 16 * i:16 * i + 16], zero_hb[:, 0:NP], zero_hb[:, 0:16], start=True, stop=True).then_inc(s, PRIME)

            def three(out, chunks):
                n = 0
                for lh, ll, rh, rl in chunks:
                    for lhs, rhs in ((lh, rh), (lh, rl), (ll, rh)):
                        n += 1
                        last = nc.tensor.matmul(out, lhs, rhs, start=n == 1, stop=n == 3 * len(chunks))
                return last

            with pe.Fori(0, B) as b:
                def x_bank(n):
                    pe.wait_ge(x_free[n % XB], b * (NX // XB) + n // XB + PRIME)
                    return xbank[n % XB]

                def x_read(n):
                    pe.wait_ge(x_free[n % XB], b * (NX // XB) + n // XB + 1 + PRIME)

                pe.wait_ge(xn_ready, b + 1)
                for k in range(KC):
                    o = x_bank(X_T + k)
                    for t in range(TT):
                        mm = nc.tensor.transpose(o[:, t * NP:(t + 1) * NP], xn[:, t, k * NP:(k + 1) * NP], ident_sb[:])
                    mm.then_inc(x_full, 1)
                x_read(X_T)
                x_read(X_T + 1)
                for t in range(TT):
                    o = x_bank(X_GATE + t)
                    for k in range(KC):
                        mm = nc.tensor.matmul(o[:, 0:2 * H * E], xnT[:, k, t * NP:(t + 1) * NP], wsel_sb[:, k, :], start=k == 0, stop=k == KC - 1)
                    mm.then_inc(x_full, 1)
                for n in range(X_GATE, X_S1T):
                    x_read(n)
                pe.wait_ge(y_free, b * 2 + PRIME)
                for y in ybank:
                    nc.tensor.matmul(y[:], zero_hb[:, 0:NP], zero_hb[:], start=True, stop=True, skip_group_check=True)

                def pair(b, p, kind):
                    it = b * HP + p
                    last_it = it - 1 if kind == INNER else b * HP + (HP - 1)

                    def w_bank(job):
                        at = place(kind, job)
                        pe.wait_ge(w_free[at % 2], b * (HP * NJ // 2) + p * (NJ // 2) + at // 2 + PRIME)
                        return wbank[at % 2]

                    def w_read(job):
                        at = place(kind, job)
                        pe.wait_ge(w_free[at % 2], b * (HP * NJ // 2) + p * (NJ // 2) + at // 2 + 1 + PRIME)

                    def project_in(t):
                        if t == 0:
                            pe.wait_ge(wqk_in, it * 16 + 16)
                        o = w_bank(("proj", 0, t))
                        for k in range(KC):
                            mm = nc.tensor.matmul(o[:, 0:NPROJ], xnT[:, k, t * NP:(t + 1) * NP], wqk_sb[:, k, :], start=k == 0, stop=k == KC - 1)
                        mm.then_inc(w_full, 1)

                    def values(j, t, of):
                        o = w_bank(("v", j, t))
                        if t == 0:
                            pe.wait_ge(wv_split[j], of + 1 + PRIME)
                            pe.wait_ge(xnT_split, b * KC + KC)
                        cols = slice(j * E * P, (j + 1) * E * P)
                        three(o[:], [(xnT_h[:, k, t * NP:(t + 1) * NP], xnT_l[:, k, t * NP:(t + 1) * NP],
                                      wv_h[:, k, cols], wv_l[:, k, cols]) for k in range(KC)]).then_inc(w_full, 1)

                    def scores(u, of):
                        j, qt, causal = unit(u)
                        pe.wait_ge(exp_done, of * UNITS + u - 1 + PRIME)
                        o = sbank[u % 2]
                        qs = slice(qt * NP, (qt + 1) * NP)
                        if causal:
                            nc.tensor.matmul(o[:, 0:(qt + 1) * NP], stackT[:, j, qs], stackT[:, 2 + j, 0:(qt + 1) * NP], start=True, stop=False)
                            mm = nc.tensor.matmul(o[:, qs], ident_hb[:], mask_sb[:], start=False, stop=True)
                        else:
                            nc.tensor.matmul(o[:], q_s[:, j, qs], k_h[:, j, :], start=True, stop=False)
                            mm = nc.tensor.matmul(o[:], q_s[:, j, qs], k_l[:, j, :], start=False, stop=True)
                        mm.then_inc(s_full, 1)

                    def turn(u, of):
                        j, qt, causal = unit(u)
                        pe.wait_ge(t_free[u % 2], of * (UNITS // 2) + u // 2 + PRIME)
                        if causal:
                            pe.wait_ge(a_scaled, of * (UNITS // 2) + u // 2 + 1)
                        else:
                            pe.wait_ge(exp_done, of * UNITS + u + 1 + PRIME)
                        for c in range(qt + 1 if causal else TT):
                            mm = nc.tensor.transpose(tbank[u % 2][:, c * NP:(c + 1) * NP], probs[:, u % 2, c * NP:(c + 1) * NP], ident_sb[:])
                        mm.then_inc(t_full, 1)

                    def gate_rows(j, of):
                        o = w_bank(("gt", j, 0))
                        pe.wait_ge(gpart_ready, of * 2 + j + 1)
                        for t in range(TT):
                            mm = nc.tensor.transpose(o.bitcast(bf16)[0:3 * E, t * NP:(t + 1) * NP], gpart[:, j, t].rearrange("q s e -> q (s e)"), ident_hb[:])
                        mm.then_inc(w_full, 1)

                    def attend(j, of):
                        o = w_bank(("pvb", j, 0))
                        pe.wait_ge(v_split, of * 2 + j + 1)
                        pe.wait_ge(t_free[0], of * (UNITS // 2) + TT * j + TT + PRIME)
                        for k in range(TT):
                            nc.tensor.matmul(o[:], v_hl[:, k, j, :], ptb_h[:, k, :], start=k == 0, stop=False)
                            mm = nc.tensor.matmul(o[:], v_hl[:, k, j, :], ptb_l[:, k, :], start=False, stop=k == TT - 1)
                        mm.then_inc(w_full, 1)

                    def attend_causal(j, of):
                        o = w_bank(("pva", j, 0))
                        pe.wait_ge(va_ready, of + 1)
                        pe.wait_ge(t_free[1], of * (UNITS // 2) + TT * j + TT + PRIME)
                        for k in range(TT):
                            mm = nc.tensor.matmul(o[0:CA, k * NP:S], va[:, k, j * CA:(j + 1) * CA], pta[:, k, k * NP:S], start=k == 0, stop=k == TT - 1)
                        mm.then_inc(w_full, 1)

                    def spread(j, e):
                        if e == 0:
                            at = place_done(kind, ("gt", j, 0))
                            pe.wait_ge(w_free[at % 2], b * (HP * NJ // 2) + p * (NJ // 2) + at // 2 + 1 + PRIME)
                        o = w_bank(("g", j, e))
                        nc.tensor.matmul(o[:], sel_sb[:, e, :], gT[:], start=True, stop=True).then_inc(w_full, 1)

                    def project(j, e, of):
                        w_read(("g", j, e))
                        if e == 0:
                            pe.wait_ge(wo_in[j], of * 16 + 16)
                        for t in range(TT):
                            mm = nc.tensor.matmul(ybank[t // 2][:, (t % 2) * D:(t % 2 + 1) * D], u_sb[:, e % 2, t * NP:(t + 1) * NP], wo_sb[:, j * EP + e, :], start=False, stop=False, skip_group_check=True)
                        mm.then_inc(o_done, 1)

                    def do(job, u):
                        name, j, n = job
                        of = last_it if of_last(job, u) else it
                        if name == "proj":
                            project_in(n)
                        elif name == "v":
                            values(j, n, of)
                        elif name == "gt":
                            gate_rows(j, of)
                        elif name == "pvb":
                            attend(j, of)
                        elif name == "pva":
                            attend_causal(j, of)
                        elif name == "g":
                            spread(j, n)
                        else:
                            project(j, n, of)

                    if kind == FIRST:
                        for t in range(TT):
                            project_in(t)
                    else:
                        for u in range(HALF_U, UNITS):
                            if u + 1 < UNITS:
                                scores(u + 1, last_it)
                            for job in beside(kind, u):
                                do(job, u)
                            turn(u, last_it)
                    if kind == TAIL:
                        for job in beside(kind, None):
                            do(job, None)
                        for u in range(HALF_U):
                            for job in beside(kind, u):
                                do(job, u)
                        return
                    pe.wait_ge(rope_ready, it + 1 + PRIME)
                    pe.wait_ge(exp_done, it * UNITS + PRIME)
                    for i in range(2):
                        for t in range(TT):
                            mm = nc.tensor.transpose(sbank[i][:, t * NP:(t + 1) * NP], raw[:, t, i * 2 * P:(i + 1) * 2 * P], ident_sb[:])
                        mm.then_inc(qk_full, 1)
                    jobs = beside(kind, None)
                    for job in jobs[:2] if kind == INNER else []:
                        do(job, None)
                    pe.wait_ge(stack_ready, it + 1)
                    for i in range(2):
                        pe.wait_ge(t_free[i], it * (UNITS // 2) + PRIME)
                        for g in range(2):
                            for t in range(TT):
                                mm = nc.tensor.transpose(tbank[i].bitcast(bf16)[0:STK, (g * TT + t) * NP:(g * TT + t + 1) * NP],
                                                         stack[:, 2 * i + g, t].rearrange("q s c -> q (s c)"), ident_hb[:])
                        mm.then_inc(stack_full, 1)
                    for job in jobs[2:] if kind == INNER else jobs:
                        do(job, None)
                    pe.wait_ge(qk_low, it * 2 + 2)
                    pe.wait_ge(stack_out, it * 2 + 2)
                    scores(0, it)
                    for u in range(HALF_U):
                        scores(u + 1, it)
                        for job in beside(kind, u):
                            do(job, u)
                        turn(u, it)

                pair(b, 0, FIRST)
                with pe.Fori(1, HP) as p:
                    pair(b, p, INNER)
                pair(b, 0, TAIL)

                pe.wait_ge(exp_done, b * (HP * UNITS) + HP * UNITS + PRIME)
                for free in t_free:
                    pe.wait_ge(free, b * (HP * UNITS // 2) + HP * UNITS // 2 + PRIME)
                pe.wait_ge(s1_ready, b + 1)
                for k in range(KC):
                    o = x_bank(X_S1T + k)
                    for t in range(TT):
                        mm = nc.tensor.transpose(o[:, t * NP:(t + 1) * NP], s1[:, t, k * NP:(k + 1) * NP], ident_sb[:])
                    mm.then_inc(x_full, 1)
                x_read(X_S1T)
                x_read(X_S1T + 1)
                for f in range(FC):
                    o = x_bank(X_F1 + f)
                    for k in range(KC):
                        mm = nc.tensor.matmul(o[:], w1_sb[:, k, f * NP:(f + 1) * NP], s1T[:, k, :], start=k == 0, stop=k == KC - 1)
                    mm.then_inc(x_full, 1)
                for n in range(X_F2 - XB, X_F2):
                    x_read(n)
                for t in range(TT):
                    o = x_bank(X_F2 + t)
                    for f in range(FC):
                        mm = nc.tensor.matmul(o[:, 0:D], hT[:, f, t * NP:(t + 1) * NP], w2_sb[:, f, :], start=f == 0, stop=f == FC - 1)
                    mm.then_inc(x_full, 1)
                pe.wait_ge(a_in, b * 16 + 16)
                for t in range(TT):
                    o = x_bank(X_WO + t)
                    for k in range(KC):
                        mm = nc.tensor.matmul(o[:, 0:D], aT[:, k, t * NP:(t + 1) * NP], w_out_sb[:, k, :], start=k == 0, stop=k == KC - 1)
                    mm.then_inc(x_full, 1)

        @block.scalar
        def _(act):
            act.wait_ge(consts_in, 12 * 16)
            for i, s in enumerate((exp_done, *t_free, *x_free, *w_free, *a_stored)):
                nc.scalar.activation(first_act[:, i:i + 1], ident_sb[0:1, 0:1], ACT.Copy).then_inc(s, PRIME)
            with act.Fori(0, B) as b:
                def roots(i):
                    act.wait_ge(var_ready, b * 3 + i + 1)
                    nc.scalar.activation(root[:], var[:], ACT.Sqrt).then_inc(root_ready, 1)

                roots(0)
                for k in range(KC):
                    act.wait_ge(x_full, b * NX + X_T + k + 1)
                    nc.scalar.activation(xnT[:, k, :], xbank[(X_T + k) % XB][:], ACT.Copy).then_inc(x_free[(X_T + k) % XB], 1)
                for t in range(TT):
                    act.wait_ge(x_full, b * NX + X_GATE + t + 1)
                    nc.scalar.activation(logit[:, t, :], xbank[(X_GATE + t) % XB][:, 0:2 * H * E], ACT.Copy).then_inc(x_free[(X_GATE + t) % XB], 1)
                for n in range(X_GATE, X_S1T):
                    act.wait_ge(x_free[n % XB], b * (NX // XB) + n // XB + 1 + PRIME)
                nc.scalar.activation(sig[:], logit[:], ACT.Sigmoid).then_inc(sig_ready, 1)
                def pair(b, p, kind):
                    it = b * HP + p
                    last_it = it - 1 if kind == INNER else b * HP + (HP - 1)

                    def drain(job, dst, part, done=None):
                        at = place(kind, job)
                        act.wait_ge(w_full, b * (HP * NJ) + p * NJ + at + 1 + PRIME)
                        nc.scalar.activation(dst, part(wbank[at % 2]), ACT.Copy).then_inc(w_free[at % 2] if done is None else done, 1)

                    def exps(u, of):
                        j, qt, causal = unit(u)
                        w = (qt + 1) * NP if causal else S
                        act.wait_ge(bias_ready, of * UNITS + u + 1)
                        act.wait_ge(t_full, of * UNITS + u - 1 + PRIME)
                        nc.scalar.activation(probs[:, u % 2, 0:w], sbank[u % 2][:, 0:w], ACT.Exp, bias=bias[:, u:u + 1],
                                             scale=CA ** -0.5 if causal else P ** -0.5,
                                             accum_out=den[:, j, int(causal), qt:qt + 1]).then_inc(exp_done, 1)

                    def turned(u, of):
                        j, qt, causal = unit(u)
                        act.wait_ge(t_full, of * UNITS + u + 1 + PRIME)
                        n = qt + 1 if causal else TT
                        dst = pta if causal else ptb_h
                        nc.scalar.activation(dst[:, 0:n, qt * NP:(qt + 1) * NP], tbank[u % 2][:, 0:n * NP].rearrange("q (c m) -> q c m", m=NP),
                                             ACT.Copy).then_inc(t_free[1] if causal else t_high, 1)

                    def store(j, of):
                        act.wait_ge(a_stored[j], of * 16 + PRIME)
                        drain(("pva", j, 0), a_st[:, j, :], lambda o: o[0:CA, :])
                        at = place(kind, ("pva", j, 0))
                        act.wait_ge(w_free[at % 2], b * (HP * NJ // 2) + p * (NJ // 2) + at // 2 + 1 + PRIME)
                        if kind == TAIL:
                            rows = a_scratch[(HP - 1) * 2 * CA + j * CA:(HP - 1) * 2 * CA + (j + 1) * CA, :]
                        else:
                            rows = a_scratch[bass.ds(p * (2 * CA) + (j - 2) * CA, CA), :]
                        act.dma_start(rows, a_st[:, j, :]).then_inc(a_stored[j], 16)

                    def do(job, u):
                        name, j, n = job
                        if name == "proj":
                            drain(job, raw[:, n, :], lambda o: o[:, 0:NPROJ])
                        elif name == "gt":
                            drain(job, gT[0:3 * E, :], lambda o: o.bitcast(bf16)[0:3 * E, 0:S])
                        elif name == "pvb":
                            drain(job, o_low[:], lambda o: o[P:NP, :], done=o_half)
                        elif name == "pva":
                            store(j, last_it)

                    if kind == FIRST:
                        for t in range(TT):
                            do(("proj", 0, t), None)
                    else:
                        for u in range(HALF_U, UNITS):
                            if u + 1 < UNITS:
                                exps(u + 1, last_it)
                            for job in beside(kind, u):
                                do(job, u)
                            turned(u, last_it)
                    if kind == TAIL:
                        for job in beside(kind, None):
                            do(job, None)
                        return
                    act.wait_ge(qk_full, it * 2 + 1)
                    for j in range(2):
                        last = nc.scalar.activation(q_s[0:P, j, :], sbank[0][j * P:(j + 1) * P, :], ACT.Copy)
                    last.then_inc(qk_high, 1)
                    act.wait_ge(qk_full, it * 2 + 2)
                    for h in range(2):
                        for j in range(2):
                            last = nc.scalar.activation(k_h[h * P:(h + 1) * P, j, :], sbank[1][j * P:(j + 1) * P, :], ACT.Copy)
                    last.then_inc(qk_high, 1)
                    jobs = beside(kind, None)
                    for job in jobs[:2] if kind == INNER else []:
                        do(job, None)
                    for i in range(2):
                        act.wait_ge(stack_full, it * 2 + i + 1)
                        nc.scalar.activation(stackT[:, 2 * i:2 * i + 2, :], tbank[i].bitcast(bf16)[0:STK, :].rearrange("q (g s) -> q g s", g=2),
                                             ACT.Copy).then_inc(stack_out, 1)
                    for job in jobs[2:] if kind == INNER else jobs:
                        do(job, None)
                    exps(0, it)
                    for u in range(HALF_U):
                        exps(u + 1, it)
                        for job in beside(kind, u):
                            do(job, u)
                        turned(u, it)

                act.wait_ge(batch_done, b + PRIME)
                pair(b, 0, FIRST)
                with act.Fori(1, HP) as p:
                    pair(b, p, INNER)
                pair(b, 0, TAIL)
                roots(1)
                for k in range(KC):
                    act.wait_ge(x_full, b * NX + X_S1T + k + 1)
                    nc.scalar.activation(s1T[:, k, :], xbank[(X_S1T + k) % XB][:], ACT.Copy).then_inc(x_free[(X_S1T + k) % XB], 1)
                for f in range(FC):
                    act.wait_ge(x_full, b * NX + X_F1 + f + 1)
                    nc.scalar.activation(hT[:, f, :], xbank[(X_F1 + f) % XB][:], ACT.Relu, bias=b1_sb[:, f:f + 1]).then_inc(x_free[(X_F1 + f) % XB], 1)
                roots(2)

        @block.vector
        def _(dve):
            BSTEPS, PSTEPS, LSTEPS = 41, 36, 15
            dve.wait_ge(consts_in, 12 * 16)
            dve.wait_ge(zeroed, 3)
            for i, s in enumerate((v_ready, rope_ready, y_free, batch_done, out_stored)):
                nc.vector.memset(first_dve[:, i:i + 1], 0.0).then_inc(s, PRIME)
            with dve.Fori(0, B) as b:
                nb = 0

                def made(ins):
                    nonlocal nb
                    nb += 1
                    ins.then_inc(batch_step, 1)
                    dve.wait_ge(batch_step, b * BSTEPS + nb)

                def normalize(dst, src, i):
                    for t in range(TT):
                        last = nc.vector.bn_stats(stats[:, t, :], src[:, t, :])
                    made(last)
                    nc.vector.memset(var[:], 0.0)
                    for t in range(TT):
                        last = nc.vector.bn_aggr(mv[:, t, :], stats[:, t, :])
                    made(last)
                    nc.vector.tensor_scalar(var[:], mv[:, :, 1], EPS, None, ALU.add).then_inc(var_ready, 1)
                    dve.wait_ge(root_ready, b * 3 + i + 1)
                    made(nc.vector.reciprocal(rstd[:], root[:]))
                    made(nc.vector.tensor_tensor(root[:], var[:], rstd[:], ALU.mult))
                    made(nc.vector.tensor_tensor(root[:], root[:], rstd[:], ALU.mult))
                    made(nc.vector.tensor_scalar(root[:], root[:], -0.5, 1.5, ALU.mult, ALU.add))
                    made(nc.vector.tensor_tensor(rstd[:], rstd[:], root[:], ALU.mult))
                    for t in range(TT):
                        last = nc.vector.tensor_scalar(dst[:, t, :], src[:, t, :], mv[:, t, 0:1], rstd[:, t:t + 1], ALU.subtract, ALU.mult)
                    return last

                def row(i):
                    return rows_sb[:, i:i + 1, :].to_broadcast([NP, TT, D])

                dve.wait_ge(x_in, b * 16 + 16)
                normalize(xn, x_sb, 0).then_inc(xn_ready, 1)
                for n in range(X_GATE, X_S1T):
                    dve.wait_ge(x_free[n % XB], b * (NX // XB) + n // XB + 1 + PRIME)
                level = gate[:].rearrange("q t (g e) -> q (t g) e", e=E)
                one = pick[:].rearrange("q t (g e) -> q (t g) e", e=E)
                two = fin[:].rearrange("q t (g e) -> q (t g) e", e=E)
                top = best[:].rearrange("q t g -> q (t g)")
                wide = [NP, TT * 2 * H, E]
                top_b = top.unsqueeze(2).to_broadcast(wide)
                rank_b = rank_sb[:, None, :].to_broadcast(wide)
                made(nc.vector.tensor_scalar(gate[:], logit[:], SIG_ONE, None, ALU.min))
                for dst in (one, two):
                    made(nc.vector.tensor_reduce(top, level, AX.X, ALU.max))
                    made(nc.vector.tensor_tensor(dst, level, top_b, ALU.is_equal))
                    made(nc.vector.tensor_tensor(dst, dst, rank_b, ALU.mult))
                    made(nc.vector.tensor_reduce(top, dst, AX.X, ALU.max))
                    made(nc.vector.tensor_tensor(dst, dst, top_b, ALU.is_equal))
                    if dst is one:
                        made(nc.vector.scalar_tensor_tensor(gate[:], pick[:], -BIG, gate[:], ALU.mult, ALU.add))
                made(nc.vector.tensor_tensor(pick[:], pick[:], fin[:], ALU.add))
                dve.wait_ge(sig_ready, b + 1)
                made(nc.vector.tensor_tensor(gate[:], sig[:], pick[:], ALU.mult))
                nc.vector.memset(peak[:], 0.0)

                def pair(b, p, kind):
                    it = b * HP + p
                    last_it = it - 1 if kind == INNER else b * HP + (HP - 1)
                    n_p = 0

                    def step(ins):
                        nonlocal n_p
                        n_p += 1
                        ins.then_inc(dve_step, 1)
                        if kind == FIRST:
                            dve.wait_ge(dve_step, it * PSTEPS + n_p)
                        else:
                            dve.wait_ge(dve_step, last_it * PSTEPS + (PSTEPS - LSTEPS) + n_p)

                    def w_filled(job):
                        at = place(kind, job)
                        dve.wait_ge(w_full, b * (HP * NJ) + p * NJ + at + 1 + PRIME)
                        return wbank[at % 2], w_free[at % 2]

                    def w_read(job):
                        at = place(kind, job)
                        dve.wait_ge(w_free[at % 2], b * (HP * NJ // 2) + p * (NJ // 2) + at // 2 + 1 + PRIME)

                    def v_gate(j, t):
                        o, free = w_filled(("v", j, t))
                        g = gates[:, t, 0, j * E:(j + 1) * E].unsqueeze(2).to_broadcast([NP, E, P])
                        nc.vector.tensor_tensor(vm[:, t % 2, :].rearrange("q (e c) -> q e c", e=E), o[:].rearrange("q (e c) -> q e c", e=E), g, ALU.mult).then_inc(free, 1)
                        w_read(("v", j, t))
                        nc.vector.tensor_reduce(v_sb[:, t, j, :], vm[:, t % 2, :].rearrange("q (e c) -> q c e", e=E), AX.X, ALU.add).then_inc(v_ready, 1)

                    def row_peak(u, of):
                        j, qt, causal = unit(u)
                        dve.wait_ge(s_full, of * UNITS + u + 1)
                        step(nc.vector.tensor_reduce(peak[:, u:u + 1], sbank[u % 2][:, 0:(qt + 1) * NP if causal else S], AX.X, ALU.max))
                        nc.vector.tensor_scalar(bias[:, u:u + 1], peak[:, u:u + 1], -(CA ** -0.5 if causal else P ** -0.5), None, ALU.mult).then_inc(bias_ready, 1)

                    def scale_probs(u, of):
                        j, qt, causal = unit(u)
                        w = (qt + 1) * NP
                        dve.wait_ge(exp_done, of * UNITS + u + 1 + PRIME)
                        step(nc.vector.reciprocal(rden[:, j, 1, qt:qt + 1], den[:, j, 1, qt:qt + 1]))
                        nc.vector.tensor_scalar(probs[:, u % 2, 0:w], probs[:, u % 2, 0:w], rden[:, j, 1, qt:qt + 1], None, ALU.mult).then_inc(a_scaled, 1)

                    def t_low(u, of):
                        qs = slice(unit(u)[1] * NP, (unit(u)[1] + 1) * NP)
                        dve.wait_ge(t_high, of * (UNITS // 2) + u // 2 + 1)
                        nc.vector.tensor_tensor(ptb_l[:, :, qs], tbank[0][:].rearrange("q (c m) -> q c m", m=NP), ptb_h.bitcast(f32)[:, :, qs], ALU.subtract).then_inc(t_free[0], 1)

                    def gate_parts(j, of):
                        dve.wait_ge(exp_done, of * UNITS + 8 * j + 7 + PRIME)
                        step(nc.vector.reciprocal(rden[:, j, 0, :], den[:, j, 0, :]))
                        step(nc.vector.tensor_tensor(gs[:, j, 0], gates[:, :, 1, j * E:(j + 1) * E], rden[:, j, 0, :].unsqueeze(2).to_broadcast([NP, TT, E]), ALU.mult))
                        step(nc.vector.tensor_copy(gpart[:, j, :, 0, :], gs[:, j, 0]))
                        step(nc.vector.tensor_tensor(gs[:, j, 1], gs[:, j, 0], gpart[:, j, :, 0, :], ALU.subtract))
                        step(nc.vector.tensor_copy(gpart[:, j, :, 1, :], gs[:, j, 1]))
                        nc.vector.tensor_tensor(gpart[:, j, :, 2, :], gs[:, j, 1], gpart[:, j, :, 1, :], ALU.subtract).then_inc(gpart_ready, 1)

                    def o_sum(j, of):
                        o, free = w_filled(("pvb", j, 0))
                        dve.wait_ge(o_half, of * 2 + j + 1)
                        nc.vector.tensor_tensor(oT[0:P, :], o[0:P, :], o_low[:], ALU.add)
                        nc.vector.tensor_tensor(oT[P:NP, :], o[0:P, :], o_low[:], ALU.add).then_inc(free, 1)

                    def u_gate(j, e, of):
                        if e == 0:
                            at = place_done(kind, ("pvb", j, 0))
                            dve.wait_ge(w_free[at % 2], b * (HP * NJ // 2) + p * (NJ // 2) + at // 2 + 1 + PRIME)
                        o, free = w_filled(("g", j, e))
                        dve.wait_ge(o_done, of * (2 * EP) + j * EP + e - 1 + PRIME)
                        nc.vector.tensor_tensor(u_sb[:, e % 2, :], o[:], oT[:], ALU.mult).then_inc(free, 1)

                    def rotate():
                        for t in (TT - 2, TT - 1):
                            w_read(("proj", 0, t))
                        head = raw[:, :, 0:NQK].rearrange("q t (g c) -> q t g c", g=4)
                        a, c = head[:, :, :, 0:HALF], head[:, :, :, HALF:NROT]
                        cos = rope_sb[:, 0].unsqueeze(2).to_broadcast([NP, TT, 4, HALF])
                        sin = rope_sb[:, 1].unsqueeze(2).to_broadcast([NP, TT, 4, HALF])
                        nc.vector.tensor_tensor(rot[:, 0], a, cos, ALU.mult)
                        nc.vector.tensor_tensor(rot[:, 1], c, sin, ALU.mult)
                        nc.vector.tensor_tensor(rot[:, 2], a, sin, ALU.mult)
                        step(nc.vector.tensor_tensor(rot[:, 3], c, cos, ALU.mult))
                        nc.vector.tensor_tensor(a, rot[:, 0], rot[:, 1], ALU.subtract)
                        nc.vector.tensor_tensor(c, rot[:, 2], rot[:, 3], ALU.add).then_inc(rope_ready, 1)

                    def do(job, u):
                        name, j, n = job
                        of = last_it if of_last(job, u) else it
                        if name == "v":
                            v_gate(j, n)
                        elif name == "pvb":
                            o_sum(j, of)
                        elif name == "g":
                            u_gate(j, n, of)

                    def tiles(units, of, end):
                        for u in units:
                            if u + 1 < end:
                                row_peak(u + 1, of)
                            if unit(u)[2]:
                                scale_probs(u, of)
                                t_low(u - 1, of)
                            for job in beside(kind, u):
                                do(job, u)
                            if u % 8 == 7:
                                gate_parts(u // 8, of)
                            if u == UNITS - 2 and kind == INNER:
                                rotate()

                    if kind == FIRST:
                        rotate()
                    else:
                        tiles(range(HALF_U, UNITS), last_it, UNITS)
                        assert n_p == LSTEPS + (kind == INNER), n_p
                    if kind == TAIL:
                        for u in (None, *range(HALF_U)):
                            for job in beside(kind, u):
                                do(job, u)
                        return
                    step(nc.vector.tensor_copy(gates[:], gate[:].rearrange("q t (v n) -> q t v n", v=2)[:, :, :, bass.ds(p * G2, G2)]))
                    dve.wait_ge(qk_high, it * 2 + 1)
                    for j in range(2):
                        last = nc.vector.tensor_tensor(q_s[P:NP, j, :], sbank[0][j * P:(j + 1) * P, :], q_s.bitcast(f32)[0:P, j, :], ALU.subtract)
                    last.then_inc(qk_low, 1)
                    dve.wait_ge(qk_high, it * 2 + 2)
                    for h in range(2):
                        for j in range(2):
                            last = nc.vector.tensor_tensor(k_l[h * P:(h + 1) * P, j, :], sbank[1][j * P:(j + 1) * P, :], k_h.bitcast(f32)[0:P, j, :], ALU.subtract)
                    last.then_inc(qk_low, 1)
                    for job in beside(kind, None):
                        do(job, None)
                    row_peak(0, it)
                    tiles(range(HALF_U), it, UNITS)
                    assert n_p == (PSTEPS - LSTEPS if kind == FIRST else PSTEPS), n_p

                pair(b, 0, FIRST)
                with dve.Fori(1, HP) as p:
                    pair(b, p, INNER)
                pair(b, 0, TAIL)

                dve.wait_ge(o_done, b * (HP * 2 * EP) + HP * 2 * EP + PRIME)
                for i, y in enumerate(ybank):
                    nc.vector.tensor_tensor(s1[:, 2 * i:2 * i + 2, :], y[:].rearrange("q (t d) -> q t d", t=2), xn[:, 2 * i:2 * i + 2, :], ALU.add).then_inc(y_free, 1)
                dve.wait_ge(y_free, b * 2 + 2 + PRIME)
                made(normalize(s1, s1, 1))
                made(nc.vector.tensor_tensor(s1[:], s1[:], row(0), ALU.mult))
                nc.vector.tensor_tensor(s1[:], s1[:], row(1), ALU.add).then_inc(s1_ready, 1)
                dve.wait_ge(s1_ready, b + 1)
                for t in range(TT):
                    dve.wait_ge(x_full, b * NX + X_F2 + t + 1)
                    nc.vector.tensor_tensor(acc[:, t, :], xbank[(X_F2 + t) % XB][:, 0:D], s1[:, t, :], ALU.add).then_inc(x_free[(X_F2 + t) % XB], 1)
                for t in range(TT):
                    dve.wait_ge(x_full, b * NX + X_WO + t + 1)
                    nc.vector.tensor_tensor(x_sb[:, t, :], xbank[(X_WO + t) % XB][:, 0:D], x_sb[:, t, :], ALU.add).then_inc(x_free[(X_WO + t) % XB], 1)
                for i in range(XB):
                    dve.wait_ge(x_free[i], b * (NX // XB) + NX // XB + PRIME)
                made(nc.vector.tensor_tensor(acc[:], acc[:], row(4), ALU.add))
                made(normalize(acc, acc, 2))
                made(nc.vector.tensor_tensor(acc[:], acc[:], row(2), ALU.mult))
                made(nc.vector.tensor_tensor(acc[:], acc[:], row(3), ALU.add))
                nc.vector.tensor_tensor(fin[:], acc[:], x_sb[:], ALU.add).then_inc(batch_done, 1)
                assert nb == BSTEPS, nb


def kernel(**inputs):
    import ml_dtypes
    import numpy as np
    import concourse.bacc as bacc
    from concourse import mybir as mb
    from concourse.bass_utils import run_bass_kernel_spmd

    a = {k: np.asarray(v) for k, v in inputs.items()}

    def chunks(w):
        return np.ascontiguousarray(w.reshape(-1, NP, w.shape[1]).transpose(1, 0, 2))

    f = "L0_ffn_"
    cols = []
    for h in range(0, H, 2):
        cols.append(np.concatenate(
            [a[f + "Wq"][h], a[f + "Wq"][h + 1], a[f + "Wk"][h], a[f + "Wk"][h + 1]]
            + [a["L0_attn_" + w][:, h * CA:(h + 2) * CA] for w in ("WQ", "WK", "WV")], axis=1))
    wqk = np.stack([chunks(c) for c in cols])
    wv = np.stack([chunks(a[f + "Wv"][h:h + 2].transpose(2, 0, 1, 3).reshape(D, 2 * E * P)) for h in range(0, H, 2)])
    wo = np.stack([chunks(a[f + "Wo"][h:h + 2].reshape(2 * E * P, D)) for h in range(0, H, 2)])
    wsel = chunks(np.concatenate([a[f + "Wsel_v"].reshape(H * E, D), a[f + "Wsel_o"].reshape(H * E, D)]).T)
    rows = np.stack([a[f + n] for n in ("ln1_g", "ln1_b", "ln2_g", "ln2_b", "b2")])
    rows = np.ascontiguousarray(np.broadcast_to(rows, (NP, 5, D)))
    inv = np.float32(10000.0) ** (-np.arange(HALF, dtype=np.float32) / np.float32(HALF))
    ang = np.arange(S, dtype=np.float32)[:, None] * inv[None, :]
    rope = np.stack([np.cos(ang), np.sin(ang)]).astype(np.float32).reshape(2, TT, NP, HALF).transpose(2, 0, 1, 3)
    bf = ml_dtypes.bfloat16
    mask = np.where(np.arange(NP)[None, :] > np.arange(NP)[:, None], -BIG, 0.0).astype(bf)
    sel = np.zeros((NP, EP, NP), bf)
    for s in range(3):
        for e in range(E):
            sel[s * E + e, e // 2, (e % 2) * P:(e % 2 + 1) * P] = 1
    rank = np.broadcast_to(np.arange(E, 0, -1, dtype=np.float32), (NP, E))
    arrays = {
        "x": a["L0_attn_x"], "wqk": wqk, "wv": wv, "wo": wo, "wsel": wsel, "w_out": chunks(a["L0_attn_WO"]),
        "w1": chunks(a[f + "W1"]), "w2": chunks(a[f + "W2"]), "b1": np.ascontiguousarray(a[f + "b1"].reshape(FC, NP).T),
        "rows": rows, "ident": np.eye(NP, dtype=np.float32), "ident_h": np.eye(NP).astype(bf), "mask": mask, "sel": sel,
        "rope": rope, "rank": rank,
    }
    arrays = {k: np.ascontiguousarray(v) for k, v in arrays.items()}
    nc = bacc.Bacc("TRN2", target_bir_lowering=False, num_devices=1)
    args = [nc.dram_tensor("in_" + k, v.shape, mb.dt.from_np(v.dtype), kind="ExternalInput").ap() for k, v in arrays.items()]
    scratch = nc.dram_tensor("a_scratch", (D, S), mb.dt.float32, kind="Internal").ap()
    out = nc.dram_tensor("out", (B, S, D), mb.dt.float32, kind="ExternalOutput").ap()
    build(nc, *args, scratch, out)
    r = run_bass_kernel_spmd(nc, [{"in_" + k: v for k, v in arrays.items()}], core_ids=[0])
    return r.results[0]["out"]
```

```python
from contextlib import ExitStack

import concourse.bass as bass
from concourse import mybir

B, S, D = 8, 512, 256
H = 16
CA = D // H
P, E = 64, 8
F = 1024
NROT = 32
HALF = NROT // 2
EPS = 1e-5
NP = 128
TT = S // NP
KC = D // NP
FC = F // NP
HP = H // 2
NQK = 4 * P
NA = 6 * CA
NPROJ = NQK + NA
EP = E // 2
G2 = 2 * E
STK = 6 * CA
BIG = 1e30
SIG_ONE = 17.4
UNITS = 16
HALF_U = 9
FILL = {9: [("pva", 0, 0), ("g", 0, 0), ("g", 0, 1)], 10: [("proj", 0, 0), ("proj", 0, 1)],
        11: [("o", 0, 0), ("proj", 0, 2)], 12: [("g", 0, 2), ("proj", 0, 3)], 13: [("o", 0, 1), ("g", 0, 3)],
        14: [("v", 1, 2), ("o", 0, 2)], 15: [("v", 1, 3), ("o", 0, 3)],
        0: [("o", 1, 0), ("v", 0, 1)], 1: [("v", 0, 2)], 2: [("g", 1, 2), ("o", 1, 1)], 3: [("g", 1, 3), ("o", 1, 2)],
        4: [("v", 0, 3)], 5: [("o", 1, 3)], 6: [("v", 1, 0)], 7: [("v", 1, 1)], 8: [("gt", 0, 0), ("pvb", 0, 0)]}
FRONT = [("gt", 1, 0), ("pva", 1, 0), ("pvb", 1, 0), ("v", 0, 0), ("g", 1, 0), ("g", 1, 1)]
FIRST, INNER, TAIL = range(3)


def of_last(job, u):
    if u is not None and u >= HALF_U:
        return job[0] != "proj"
    return job[0] in ("gt", "pvb", "pva", "g", "o") and job[1] == 1


ORDER = ([(j, of_last(j, u)) for u in range(HALF_U, UNITS) for j in FILL[u]] + [(j, of_last(j, None)) for j in FRONT]
         + [(j, of_last(j, u)) for u in range(HALF_U) for j in FILL[u]])
JOBS = [(j, last) for j, last in ORDER if j[0] != "o"]
NJ = len(JOBS)
LATE = [j for j, last in JOBS if last]
EARLY = [j for j, last in JOBS if not last]
START, NEXT, END = range(3)
XB = 4
X_START = [("xnT", 0), ("xnT", 1), ("gate", 0), ("gate", 1)]
X_OUT = [("aT", 0), ("aT", 1), ("wo", 0), ("wo", 1)]
X_JOBS = {START: X_START,
          NEXT: X_OUT + X_START + [("s1T", 0), ("s1T", 1)] + [("f1", f) for f in range(FC)] + [("f2", 0), ("f2", 1)],
          END: X_OUT + [("s1T", 0), ("s1T", 1)] + [("f1", f) for f in range(FC)] + [("f2", 0), ("f2", 1)]}
NX = len(X_JOBS[NEXT])
PRIME = 6


def unit(u):
    return u // 8, (u % 8) // 2, u % 2 == 1


def place(kind, job):
    if kind == FIRST:
        return EARLY.index(job)
    if kind == TAIL:
        return HP * NJ - len(LATE) + LATE.index(job)
    return [j for j, _ in JOBS].index(job) - len(LATE)


def place_done(kind, job):
    if job[1] == 1:
        return place(kind, job)
    return (HP * NJ if kind == TAIL else 0) + [j for j, _ in JOBS].index(job) - len(LATE) - NJ


def x_place(kind, job):
    return X_JOBS[kind].index(job) - (XB if kind == START else 0)


def beside(kind, u):
    jobs = FRONT if u is None else FILL[u]
    return [j for j in jobs if kind == INNER or of_last(j, u) == (kind == TAIL)]


def build(nc, x, wqk, wv, wo, wsel, w_out, w1, w2, b1, rows, ident, ident_h, mask, sel, rope, rank, out):
    f32, bf16 = mybir.dt.float32, mybir.dt.bfloat16
    f32r = mybir.dt.float32r
    ALU, ACT, AX = mybir.AluOpType, mybir.ActivationFunctionType, mybir.AxisListType
    x_v = x.rearrange("b (t p) d -> b p t d", p=NP)
    out_v = out.rearrange("b (t p) d -> b p t d", p=NP)
    with ExitStack() as ctx:
        def sb(name, shape, dt=f32):
            return ctx.enter_context(nc.sbuf_tensor(name, shape, dt))

        def sem(name):
            return ctx.enter_context(nc.semaphore(name))

        first_dve = sb("first_dve", [1, 8])
        first_pool = sb("first_pool", [1, 8])
        primer = sb("primer", [1, 8])
        first_act = sb("first_act", [1, 16])
        ident_sb = sb("ident_sb", [NP, NP])
        ident_hb = sb("ident_hb", [NP, NP], bf16)
        mask_sb = sb("mask_sb", [NP, NP], bf16)
        sel_sb = sb("sel_sb", [NP, EP, NP], bf16)
        rope_sb = sb("rope_sb", [NP, 2, TT, HALF])
        rank_sb = sb("rank_sb", [NP, E])
        rows_sb = sb("rows_sb", [NP, 5, D])
        b1_sb = sb("b1_sb", [NP, FC])
        wsel_sb = sb("wsel_sb", [NP, KC, 2 * H * E])
        w_out_sb = sb("w_out_sb", [NP, KC, D])
        w1_sb = sb("w1_sb", [NP, KC, F])
        w2_sb = sb("w2_sb", [NP, FC, D])
        zero_hb = sb("zero_hb", [NP, S], bf16)
        wqk_sb = sb("wqk_sb", [NP, KC, NPROJ])
        wv_sb = sb("wv_sb", [NP, KC, 2 * E * P])
        wv_h = sb("wv_h", [NP, KC, 2 * E * P], f32r)
        wv_l = sb("wv_l", [NP, KC, 2 * E * P], f32r)
        wo_sb = sb("wo_sb", [NP, 2 * EP, D])
        x_sb = sb("x_sb", [NP, TT, D])
        xn = sb("xn", [NP, TT, D])
        xnT = sb("xnT", [NP, KC, S])
        xnT_h = sb("xnT_h", [NP, KC, S], f32r)
        xnT_l = sb("xnT_l", [NP, KC, S], f32r)
        stats = sb("stats", [NP, TT, 6])
        mv = sb("mv", [NP, TT, 2])
        var = sb("var", [NP, TT])
        root = sb("root", [NP, TT])
        rstd = sb("rstd", [NP, TT])
        logit = sb("logit", [NP, TT, 2 * H * E])
        sig = sb("sig", [NP, TT, 2 * H * E])
        gate = sb("gate", [NP, TT, 2 * H * E])
        pick = sb("pick", [NP, TT, 2 * H * E])
        best = sb("best", [NP, TT, 2 * H])
        hT = sb("hT", [NP, FC, S])
        a_sb = sb("a_sb", [NP, TT, D])
        acc = sb("acc", [NP, TT, D])
        resid = sb("resid", [NP, TT, D])
        fin = sb("fin", [NP, TT, D])
        raw = sb("raw", [NP, TT, NPROJ])
        rot = sb("rot", [NP, 4, TT, 4, HALF])
        q_s = sb("q_s", [NP, 2, S], f32r)
        k_h = sb("k_h", [NP, 2, S], f32r)
        k_l = sb("k_l", [NP, 2, S], f32r)
        part = sb("part", [NP, 4, TT, 3, CA], bf16)
        rest = sb("rest", [NP, 2, 4, TT, CA])
        stack = sb("stack", [NP, 4, TT, 6, CA], bf16)
        stackT = sb("stackT", [STK, 4, S], bf16)
        gates = sb("gates", [NP, TT, 2, G2])
        vm = sb("vm", [NP, 2, E * P])
        v_sb = sb("v_sb", [NP, TT, 2, P])
        peak = sb("peak", [NP, UNITS])
        bias = sb("bias", [NP, UNITS])
        den = sb("den", [NP, 2, 2, TT])
        rden = sb("rden", [NP, 2, 2, TT])
        probs = sb("probs", [NP, 2, S])
        v_hl = sb("v_hl", [NP, TT, 2, 2 * P], f32r)
        ptb_h = sb("ptb_h", [NP, TT, S], f32r)
        ptb_l = sb("ptb_l", [NP, TT, S], f32r)
        o_low = sb("o_low", [P, S])
        pta = hT[:, 0:TT, :]
        gs = sb("gs", [NP, 2, 3, TT, E])
        gpart = sb("gpart", [NP, 2, TT, 3, E], bf16)
        gT = sb("gT", [NP, S], bf16)
        oT = sb("oT", [NP, S])
        u_sb = sb("u_sb", [NP, 2, S])
        va = sb("va", [NP, TT, 2 * CA])
        s1 = a_sb
        s1T = probs
        aT = vm

        bank = [ctx.enter_context(nc.psum_tensor(f"bank{i}", [NP, S], f32)) for i in range(8)]
        ybank = [bank[0], bank[1]]
        sbank = [bank[2], bank[3]]
        tbank = [bank[4], bank[5]]
        wbank = [bank[6], bank[7]]
        xbank = bank[2:6]

        consts_in = sem("consts_in")
        x_in = sem("x_in")
        wqk_in = sem("wqk_in")
        wv_in = [sem("wv_in0"), sem("wv_in1")]
        wo_in = [sem("wo_in0"), sem("wo_in1")]
        out_stored = sem("out_stored")
        zeroed = sem("zeroed")
        x_full = sem("x_full")
        x_free = [sem(f"x_free{i}") for i in range(XB)]
        xn_ready = sem("xn_ready")
        var_ready = sem("var_ready")
        root_ready = sem("root_ready")
        sig_ready = sem("sig_ready")
        s1_ready = sem("s1_ready")
        resid_ready = sem("resid_ready")
        acc_ready = sem("acc_ready")
        finish_step = sem("finish_step")
        batch_done = sem("batch_done")
        w_full = sem("w_full")
        w_free = [sem("w_free0"), sem("w_free1")]
        rope_ready = sem("rope_ready")
        va_ready = sem("va_ready")
        stack_ready = sem("stack_ready")
        v_ready = sem("v_ready")
        s_full = sem("s_full")
        bias_ready = sem("bias_ready")
        exp_done = sem("exp_done")
        t_full = sem("t_full")
        t_free = [sem("t_free_expert"), sem("t_free_causal")]
        t_high = sem("t_high")
        o_half = sem("o_half")
        qk_full, qk_high, qk_low = sem("qk_full"), sem("qk_high"), sem("qk_low")
        stack_full, stack_out = sem("stack_full"), sem("stack_out")
        wv_split = [sem("wv_split0"), sem("wv_split1")]
        xnT_high = sem("xnT_high")
        xnT_split = sem("xnT_split")
        v_split = sem("v_split")
        gpart_ready = sem("gpart_ready")
        o_done = sem("o_done")
        dve_step = sem("dve_step")
        batch_step = sem("batch_step")
        pool_step = sem("pool_step")

        block = ctx.enter_context(nc.Block())

        @block.sync
        def _(sp):
            for dst, src in ((ident_sb[:], ident), (ident_hb[:], ident_h), (mask_sb[:], mask), (sel_sb[:], sel),
                             (rope_sb[:], rope), (rank_sb[:], rank), (b1_sb[:], b1), (rows_sb[:], rows),
                             (wsel_sb[:], wsel), (w_out_sb[:], w_out), (w1_sb[:], w1), (w2_sb[:], w2)):
                sp.dma_start(dst, src).then_inc(consts_in, 16)

            def load_x(b):
                sp.dma_start(x_sb[:], x_v[bass.ds(b, 1), :, :, :].rearrange("b p t d -> p (b t) d")).then_inc(x_in, 16)

            def load_pair(b, p):
                it = b * HP + p
                sp.wait_ge(rope_ready, it + PRIME)
                sp.dma_start(wqk_sb[:], wqk[bass.ds(p, 1), :, :, :].rearrange("o q k n -> (o q) k n")).then_inc(wqk_in, 16)
                for j in range(2):
                    sp.wait_ge(wv_split[j], it + PRIME)
                    sp.dma_start(wv_sb[:, :, j * E * P:(j + 1) * E * P], wv[bass.ds(p, 1), :, :, j * E * P:(j + 1) * E * P].rearrange("o q k n -> (o q) k n")).then_inc(wv_in[j], 16)
                for j in range(2):
                    sp.wait_ge(o_done, it * (2 * EP) + (j - 1) * EP + PRIME)
                    sp.dma_start(wo_sb[:, j * EP:(j + 1) * EP, :], wo[bass.ds(p, 1), :, j * EP:(j + 1) * EP, :].rearrange("o q k n -> (o q) k n")).then_inc(wo_in[j], 16)

            def store(b):
                sp.wait_ge(batch_done, b + 1 + PRIME)
                sp.dma_start(out_v[bass.ds(b, 1), :, :, :].rearrange("b p t d -> p (b t) d"), fin[:]).then_inc(out_stored, 16)

            load_x(0)
            with sp.Fori(0, HP) as p:
                load_pair(0, p)
            with sp.Fori(1, B) as b:
                sp.wait_ge(resid_ready, b + PRIME)
                load_x(b)
                load_pair(b, 0)
                store(b - 1)
                with sp.Fori(1, HP) as p:
                    load_pair(b, p)
            store(B - 1)
            sp.wait_ge(out_stored, B * 16 + PRIME)

        @block.gpsimd
        def _(pool):
            nc.gpsimd.memset(zero_hb[:], 0.0).then_inc(zeroed, 1)
            nc.gpsimd.memset(first_pool[:], 0.0).then_inc(zeroed, 1)
            for i, s in enumerate(wv_split):
                nc.gpsimd.memset(primer[:, i:i + 1], 0.0).then_inc(s, PRIME)
            nc.gpsimd.memset(gT[:], 0.0).then_inc(zeroed, 1)
            def finish(b):
                pool.wait_ge(acc_ready, b + 1)
                for n, (dst, x, y, op) in enumerate(((acc, acc, rows_sb[:, 2:3, :].to_broadcast([NP, TT, D]), ALU.mult),
                                                     (acc, acc, rows_sb[:, 3:4, :].to_broadcast([NP, TT, D]), ALU.add))):
                    nc.gpsimd.tensor_tensor(dst[:], x[:], y, op).then_inc(finish_step, 1)
                    pool.wait_ge(finish_step, b * 2 + n + 1)
                pool.wait_ge(out_stored, b * 16 + PRIME)
                nc.gpsimd.tensor_tensor(fin[:], acc[:], resid[:], ALU.add).then_inc(batch_done, 1)

            def batch(b, first):
                def w_read(kind, b, p, job):
                    at = place(kind, job)
                    pool.wait_ge(w_free[at % 2], b * (HP * NJ // 2) + p * (NJ // 2) + at // 2 + 1 + PRIME)

                def pair(b, p, kind):
                    it = b * HP + p
                    last_it = it - 1 if kind == INNER else b * HP + (HP - 1)
                    n = 0
                    STEPS = 8

                    def made(ins):
                        nonlocal n
                        n += 1
                        ins.then_inc(pool_step, 1)
                        pool.wait_ge(pool_step, (last_it + 1 if kind != FIRST else it) * STEPS - (kind != FIRST) + n)

                    def split_wv(j):
                        cols = slice(j * E * P, (j + 1) * E * P)
                        pool.wait_ge(wv_in[j], it * 16 + 16)
                        pool.wait_ge(v_ready, it * (2 * TT) + (j - 1) * TT + PRIME)
                        made(nc.gpsimd.tensor_tensor(wv_h[:, :, cols], wv_sb[:, :, cols], zero_hb[:, None, :].to_broadcast([NP, KC, E * P]), ALU.add))
                        nc.gpsimd.tensor_tensor(wv_l[:, :, cols], wv_sb[:, :, cols], wv_h.bitcast(f32)[:, :, cols], ALU.subtract).then_inc(wv_split[j], 1)

                    def split_v(j, of):
                        pool.wait_ge(v_ready, of * (2 * TT) + TT * j + TT + PRIME)
                        made(nc.gpsimd.tensor_tensor(v_hl[:, :, j, 0:P], v_sb[:, :, j, :], zero_hb[:, 0:TT * P].rearrange("q (t c) -> q t c", t=TT), ALU.add))
                        nc.gpsimd.tensor_tensor(v_hl[:, :, j, P:2 * P], v_sb[:, :, j, :], v_hl.bitcast(f32)[:, :, j, 0:P], ALU.subtract).then_inc(v_split, 1)

                    if kind == TAIL:
                        split_v(1, last_it)
                        return
                    split_wv(0)
                    for t in (TT - 2, TT - 1):
                        w_read(kind, b, p, ("proj", 0, t))
                    src = raw[:, :, NQK:NQK + 4 * CA].rearrange("q t (g c) -> q g t c", g=4)
                    zeros = zero_hb[:, 0:4 * TT * CA].rearrange("q (g t c) -> q g t c", g=4, t=TT)
                    made(nc.gpsimd.tensor_tensor(part[:, :, :, 0, :], src, zeros, ALU.add))
                    made(nc.gpsimd.tensor_tensor(rest[:, 0], src, part[:, :, :, 0, :], ALU.subtract))
                    made(nc.gpsimd.tensor_tensor(part[:, :, :, 1, :], rest[:, 0], zeros, ALU.add))
                    made(nc.gpsimd.tensor_tensor(part[:, :, :, 2, :], rest[:, 0], part[:, :, :, 1, :], ALU.subtract))
                    pq = part[:, 0:2].rearrange("q g t s c -> q (g t) s c")
                    pk = part[:, 2:4].rearrange("q g t s c -> q (g t) s c")
                    sq = stack[:, 0:2].rearrange("q g t s c -> q (g t) s c")
                    sk = stack[:, 2:4].rearrange("q g t s c -> q (g t) s c")
                    nc.gpsimd.tensor_tensor(sq[:, :, 0:3, :], pq[:, :, 0:1, :].to_broadcast([NP, 2 * TT, 3, CA]),
                                            zero_hb[:, 0:6 * TT * CA].rearrange("q (g s c) -> q g s c", s=3, c=CA), ALU.add)
                    nc.gpsimd.tensor_copy(sq[:, :, 3:5, :], pq[:, :, 1:2, :].to_broadcast([NP, 2 * TT, 2, CA]))
                    nc.gpsimd.tensor_copy(sq[:, :, 5, :], pq[:, :, 2, :])
                    nc.gpsimd.tensor_copy(sk[:, :, 0:3, :], pk)
                    nc.gpsimd.tensor_copy(sk[:, :, 3:5, :], pk[:, :, 0:2, :])
                    nc.gpsimd.tensor_copy(sk[:, :, 5, :], pk[:, :, 0, :]).then_inc(stack_ready, 1)
                    if kind == FIRST and not first:
                        finish(b - 1)
                    if kind == INNER:
                        split_v(1, last_it)
                    split_wv(1)
                    if kind == INNER:
                        w_read(kind, b, p, ("pva", 1, 0))
                    nc.gpsimd.tensor_tensor(va[:], raw[:, :, NQK + 4 * CA:], zero_hb[:, 0:TT * 2 * CA].rearrange("q (t c) -> q t c", t=TT), ALU.add).then_inc(va_ready, 1)
                    split_v(0, it)
                    assert n == STEPS - (kind == FIRST), n

                for k in range(KC):
                    at, last = (x_place(START, ("xnT", k)), b) if first else (x_place(NEXT, ("xnT", k)), b - 1)
                    pool.wait_ge(x_free[at % XB], last * (NX // XB) + 1 + at // XB + 1 + PRIME)
                    nc.gpsimd.tensor_tensor(xnT_h[:, k, :], xnT[:, k, :], zero_hb[:], ALU.add).then_inc(xnT_high, 1)
                    pool.wait_ge(xnT_high, b * KC + k + 1)
                    nc.gpsimd.tensor_tensor(xnT_l[:, k, :], xnT[:, k, :], xnT_h.bitcast(f32)[:, k, :], ALU.subtract).then_inc(xnT_split, 1)
                pair(b, 0, FIRST)
                with pool.Fori(1, HP) as p:
                    pair(b, p, INNER)
                pair(b, 0, TAIL)

            batch(0, True)
            with pool.Fori(1, B) as b:
                batch(b, False)
            finish(B - 1)

        @block.tensor
        def _(pe):
            pe.wait_ge(consts_in, 12 * 16)
            pe.wait_ge(zeroed, 3)
            for i, s in enumerate((w_full, o_done, t_full)):
                nc.tensor.matmul(bank[7][:, 16 * i:16 * i + 16], zero_hb[:, 0:NP], zero_hb[:, 0:16], start=True, stop=True).then_inc(s, PRIME)

            def three(out, chunks):
                n = 0
                for lh, ll, rh, rl in chunks:
                    for lhs, rhs in ((lh, rh), (lh, rl), (ll, rh)):
                        n += 1
                        last = nc.tensor.matmul(out, lhs, rhs, start=n == 1, stop=n == 3 * len(chunks))
                return last

            def x_bank(b, kind, job):
                at = x_place(kind, job)
                pe.wait_ge(x_free[at % XB], b * (NX // XB) + 1 + at // XB + PRIME)
                return xbank[at % XB]

            def x_read(b, kind, name):
                for i in range(2):
                    at = x_place(kind, (name, i))
                    pe.wait_ge(x_free[at % XB], b * (NX // XB) + 1 + at // XB + 1 + PRIME)

            def turn_rows(b, kind, name, src):
                for k in range(KC):
                    o = x_bank(b, kind, (name, k))
                    for t in range(TT):
                        mm = nc.tensor.transpose(o[:, t * NP:(t + 1) * NP], src[:, t, k * NP:(k + 1) * NP], ident_sb[:])
                    mm.then_inc(x_full, 1)

            def rows_of(b, kind, name, lhs, w, chunks, which=(0, 1)):
                for i in which:
                    o = x_bank(b, kind, (name, i))
                    for t in (2 * i, 2 * i + 1):
                        for k in range(chunks):
                            mm = nc.tensor.matmul(o[:, (t % 2) * D:(t % 2 + 1) * D], lhs[:, k, t * NP:(t + 1) * NP], w[:, k, :], start=k == 0, stop=k == chunks - 1)
                    mm.then_inc(x_full, 1)

            def hidden(b, kind, f):
                o = x_bank(b, kind, ("f1", f))
                for k in range(KC):
                    mm = nc.tensor.matmul(o[:], w1_sb[:, k, f * NP:(f + 1) * NP], s1T[:, k, :], start=k == 0, stop=k == KC - 1)
                mm.then_inc(x_full, 1)

            def start_sums():
                for y in ybank:
                    nc.tensor.matmul(y[:], zero_hb[:, 0:NP], zero_hb[:], start=True, stop=False, skip_group_check=True)
                for t in range(TT):
                    nc.tensor.matmul(ybank[t // 2][:, (t % 2) * D:(t % 2 + 1) * D], ident_sb[:], xn[:, t, :], start=False, stop=False, skip_group_check=True)

            def causal_out(b):
                pe.wait_ge(exp_done, b * (HP * UNITS) + HP * UNITS + PRIME)
                for free in t_free:
                    pe.wait_ge(free, b * (HP * UNITS // 2) + HP * UNITS // 2 + PRIME)
                at = place(TAIL, ("pva", 1, 0))
                pe.wait_ge(w_free[at % 2], b * (HP * NJ // 2) + at // 2 + 1 + PRIME)
                turn_rows(b, NEXT, "aT", a_sb)
                x_read(b, NEXT, "aT")
                rows_of(b, NEXT, "wo", aT, w_out_sb, KC)

            def norm_turned(b, kind, of):
                pe.wait_ge(xn_ready, of + 1)
                turn_rows(b, kind, "xnT", xn)

            def gate_logits(b, kind):
                x_read(b, kind, "xnT")
                rows_of(b, kind, "gate", xnT, wsel_sb, KC)

            def between(b, kind):
                if kind == NEXT:
                    norm_turned(b, kind, b + 1)
                    gate_logits(b, kind)
                pe.wait_ge(s1_ready, b + 1)
                turn_rows(b, kind, "s1T", s1)
                x_read(b, kind, "s1T")
                for f in range(FC):
                    hidden(b, kind, f)

            def second_layer(b, kind, half):
                for f in range(FC - XB, FC):
                    at = x_place(kind, ("f1", f))
                    pe.wait_ge(x_free[at % XB], b * (NX // XB) + 1 + at // XB + 1 + PRIME)
                rows_of(b, kind, "f2", hT, w2_sb, FC, (half,))

            def pair(b, p, kind, after_last=False):
                it = b * HP + p
                last_it = it - 1 if kind == INNER else b * HP + (HP - 1)

                def w_bank(job):
                    at = place(kind, job)
                    pe.wait_ge(w_free[at % 2], b * (HP * NJ // 2) + p * (NJ // 2) + at // 2 + PRIME)
                    return wbank[at % 2]

                def w_read(job):
                    at = place(kind, job)
                    pe.wait_ge(w_free[at % 2], b * (HP * NJ // 2) + p * (NJ // 2) + at // 2 + 1 + PRIME)

                def project_in(t):
                    if t == 0:
                        pe.wait_ge(wqk_in, it * 16 + 16)
                    o = w_bank(("proj", 0, t))
                    for k in range(KC):
                        mm = nc.tensor.matmul(o[:, 0:NPROJ], xnT[:, k, t * NP:(t + 1) * NP], wqk_sb[:, k, :], start=k == 0, stop=k == KC - 1)
                    mm.then_inc(w_full, 1)

                def values(j, t, of):
                    o = w_bank(("v", j, t))
                    if t == 0:
                        pe.wait_ge(wv_split[j], of + 1 + PRIME)
                        pe.wait_ge(xnT_split, b * KC + KC)
                    cols = slice(j * E * P, (j + 1) * E * P)
                    three(o[:], [(xnT_h[:, k, t * NP:(t + 1) * NP], xnT_l[:, k, t * NP:(t + 1) * NP],
                                  wv_h[:, k, cols], wv_l[:, k, cols]) for k in range(KC)]).then_inc(w_full, 1)

                def scores(u, of):
                    j, qt, causal = unit(u)
                    pe.wait_ge(exp_done, of * UNITS + u - 1 + PRIME)
                    o = sbank[u % 2]
                    qs = slice(qt * NP, (qt + 1) * NP)
                    if causal:
                        nc.tensor.matmul(o[:, 0:(qt + 1) * NP], stackT[:, j, qs], stackT[:, 2 + j, 0:(qt + 1) * NP], start=True, stop=False)
                        mm = nc.tensor.matmul(o[:, qs], ident_hb[:], mask_sb[:], start=False, stop=True)
                    else:
                        nc.tensor.matmul(o[:], q_s[:, j, qs], k_h[:, j, :], start=True, stop=False)
                        mm = nc.tensor.matmul(o[:], q_s[:, j, qs], k_l[:, j, :], start=False, stop=True)
                    mm.then_inc(s_full, 1)

                def turn(u, of):
                    j, qt, causal = unit(u)
                    pe.wait_ge(t_free[u % 2], of * (UNITS // 2) + u // 2 + PRIME)
                    pe.wait_ge(exp_done, of * UNITS + u + 1 + PRIME)
                    for c in range(qt + 1 if causal else TT):
                        mm = nc.tensor.transpose(tbank[u % 2][:, c * NP:(c + 1) * NP], probs[:, u % 2, c * NP:(c + 1) * NP], ident_sb[:])
                    mm.then_inc(t_full, 1)

                def gate_rows(j, of):
                    o = w_bank(("gt", j, 0))
                    pe.wait_ge(gpart_ready, of * 2 + j + 1)
                    for t in range(TT):
                        mm = nc.tensor.transpose(o.bitcast(bf16)[0:3 * E, t * NP:(t + 1) * NP], gpart[:, j, t].rearrange("q s e -> q (s e)"), ident_hb[:])
                    mm.then_inc(w_full, 1)

                def attend(j, of):
                    o = w_bank(("pvb", j, 0))
                    pe.wait_ge(v_split, of * 2 + j + 1)
                    pe.wait_ge(t_free[0], of * (UNITS // 2) + TT * j + TT + PRIME)
                    for k in range(TT):
                        nc.tensor.matmul(o[:], v_hl[:, k, j, :], ptb_h[:, k, :], start=k == 0, stop=False)
                        mm = nc.tensor.matmul(o[:], v_hl[:, k, j, :], ptb_l[:, k, :], start=False, stop=k == TT - 1)
                    mm.then_inc(w_full, 1)

                def attend_causal(j, of):
                    o = w_bank(("pva", j, 0))
                    pe.wait_ge(va_ready, of + 1)
                    pe.wait_ge(t_free[1], of * (UNITS // 2) + TT * j + TT + PRIME)
                    for qt in range(TT):
                        for k in range(qt + 1):
                            mm = nc.tensor.matmul(o[:, qt * CA:(qt + 1) * CA], pta[:, k, qt * NP:(qt + 1) * NP], va[:, k, j * CA:(j + 1) * CA], start=k == 0, stop=k == qt)
                    mm.then_inc(w_full, 1)

                def spread(j, e):
                    if e == 0:
                        at = place_done(kind, ("gt", j, 0))
                        pe.wait_ge(w_free[at % 2], b * (HP * NJ // 2) + p * (NJ // 2) + at // 2 + 1 + PRIME)
                    o = w_bank(("g", j, e))
                    nc.tensor.matmul(o[:], sel_sb[:, e, :], gT[:], start=True, stop=True).then_inc(w_full, 1)

                def project(j, e, of):
                    w_read(("g", j, e))
                    if e == 0:
                        pe.wait_ge(wo_in[j], of * 16 + 16)
                    for t in range(TT):
                        mm = nc.tensor.matmul(ybank[t // 2][:, (t % 2) * D:(t % 2 + 1) * D], u_sb[:, e % 2, t * NP:(t + 1) * NP], wo_sb[:, j * EP + e, :], start=False, stop=False, skip_group_check=True)
                    mm.then_inc(o_done, 1)

                def do(job, u):
                    name, j, n = job
                    of = last_it if of_last(job, u) else it
                    if name == "proj":
                        project_in(n)
                    elif name == "v":
                        values(j, n, of)
                    elif name == "gt":
                        gate_rows(j, of)
                    elif name == "pvb":
                        attend(j, of)
                    elif name == "pva":
                        attend_causal(j, of)
                    elif name == "g":
                        spread(j, n)
                    else:
                        project(j, n, of)

                if kind == FIRST:
                    for t in range(TT):
                        project_in(t)
                    if after_last:
                        second_layer(b - 1, NEXT, 0)
                else:
                    for u in range(HALF_U, UNITS):
                        if u + 1 < UNITS:
                            scores(u + 1, last_it)
                        for job in beside(kind, u):
                            do(job, u)
                        turn(u, last_it)
                if kind == TAIL:
                    for job in beside(kind, None):
                        do(job, None)
                    causal_out(b)
                    for u in range(HALF_U):
                        for job in beside(kind, u):
                            do(job, u)
                    return
                pe.wait_ge(rope_ready, it + 1 + PRIME)
                pe.wait_ge(exp_done, it * UNITS + PRIME)
                if kind == FIRST:
                    for free in x_free[0:2]:
                        pe.wait_ge(free, b * (NX // XB) + 1 + PRIME)
                for i in range(2):
                    for t in range(TT):
                        mm = nc.tensor.transpose(sbank[i][:, t * NP:(t + 1) * NP], raw[:, t, i * 2 * P:(i + 1) * 2 * P], ident_sb[:])
                    mm.then_inc(qk_full, 1)
                if kind == FIRST:
                    if after_last:
                        second_layer(b - 1, NEXT, 1)
                    start_sums()
                    for free in x_free[2:4]:
                        pe.wait_ge(free, b * (NX // XB) + 1 + PRIME)
                jobs = beside(kind, None)
                for job in jobs[:2] if kind == INNER else []:
                    do(job, None)
                pe.wait_ge(stack_ready, it + 1)
                for i in range(2):
                    pe.wait_ge(t_free[i], it * (UNITS // 2) + PRIME)
                    for g in range(2):
                        for t in range(TT):
                            mm = nc.tensor.transpose(tbank[i].bitcast(bf16)[0:STK, (g * TT + t) * NP:(g * TT + t + 1) * NP],
                                                     stack[:, 2 * i + g, t].rearrange("q s c -> q (s c)"), ident_hb[:])
                    mm.then_inc(stack_full, 1)
                for job in jobs[2:] if kind == INNER else jobs:
                    do(job, None)
                pe.wait_ge(qk_low, it * 2 + 2)
                pe.wait_ge(stack_out, it * 2 + 2)
                scores(0, it)
                for u in range(HALF_U):
                    scores(u + 1, it)
                    for job in beside(kind, u):
                        do(job, u)
                    turn(u, it)

            def pairs(b):
                with pe.Fori(1, HP) as p:
                    pair(b, p, INNER)
                pair(b, 0, TAIL)

            norm_turned(0, START, 0)
            gate_logits(0, START)
            pair(0, 0, FIRST)
            with pe.Fori(0, B - 1) as b:
                pairs(b)
                between(b, NEXT)
                pair(b + 1, 0, FIRST, after_last=True)
            pairs(B - 1)
            between(B - 1, END)
            for half in range(2):
                second_layer(B - 1, END, half)

        @block.scalar
        def _(act):
            act.wait_ge(consts_in, 12 * 16)
            for i, s in enumerate((exp_done, *t_free, *x_free, *w_free)):
                nc.scalar.activation(first_act[:, i:i + 1], ident_sb[0:1, 0:1], ACT.Copy).then_inc(s, PRIME)
            def roots(n):
                act.wait_ge(var_ready, n + 1)
                nc.scalar.activation(root[:], var[:], ACT.Sqrt).then_inc(root_ready, 1)

            def x_out(b, kind, job, dst, func=ACT.Copy, part=lambda o: o[:], **kw):
                at = x_place(kind, job)
                act.wait_ge(x_full, b * NX + XB + at + 1)
                nc.scalar.activation(dst, part(xbank[at % XB]), func, **kw).then_inc(x_free[at % XB], 1)

            def turned_out(b, kind, name, dst):
                for k in range(KC):
                    x_out(b, kind, (name, k), dst[:, k, :])

            def gates_out(b, kind):
                for i in range(TT // 2):
                    x_out(b, kind, ("gate", i), logit[:, 2 * i:2 * i + 2, :], part=lambda o: o[:].rearrange("q (t n) -> q t n", t=2))
                for i in range(TT // 2):
                    at = x_place(kind, ("gate", i))
                    act.wait_ge(x_free[at % XB], b * (NX // XB) + 1 + at // XB + 1 + PRIME)
                nc.scalar.activation(sig[:], logit[:], ACT.Sigmoid).then_inc(sig_ready, 1)

            def between(b, kind):
                if kind == NEXT:
                    roots(b * 3 + 1)
                    turned_out(b, kind, "xnT", xnT)
                    roots(b * 3 + 2)
                    gates_out(b, kind)
                else:
                    roots(b * 3 + 1)
                turned_out(b, kind, "s1T", s1T)
                for f in range(FC):
                    x_out(b, kind, ("f1", f), hT[:, f, :], func=ACT.Relu, bias=b1_sb[:, f:f + 1])

            def pair(b, p, kind, after_last=False):
                it = b * HP + p
                last_it = it - 1 if kind == INNER else b * HP + (HP - 1)

                def drain(job, dst, part, done=None):
                    at = place(kind, job)
                    act.wait_ge(w_full, b * (HP * NJ) + p * NJ + at + 1 + PRIME)
                    nc.scalar.activation(dst, part(wbank[at % 2]), ACT.Copy).then_inc(w_free[at % 2] if done is None else done, 1)

                def exps(u, of):
                    j, qt, causal = unit(u)
                    w = (qt + 1) * NP if causal else S
                    act.wait_ge(bias_ready, of * UNITS + u + 1)
                    act.wait_ge(t_full, of * UNITS + u - 1 + PRIME)
                    nc.scalar.activation(probs[:, u % 2, 0:w], sbank[u % 2][:, 0:w], ACT.Exp, bias=bias[:, u:u + 1],
                                         scale=CA ** -0.5 if causal else P ** -0.5,
                                         accum_out=den[:, j, int(causal), qt:qt + 1]).then_inc(exp_done, 1)

                def turned(u, of):
                    j, qt, causal = unit(u)
                    act.wait_ge(t_full, of * UNITS + u + 1 + PRIME)
                    n = qt + 1 if causal else TT
                    dst = pta if causal else ptb_h
                    nc.scalar.activation(dst[:, 0:n, qt * NP:(qt + 1) * NP], tbank[u % 2][:, 0:n * NP].rearrange("q (c m) -> q c m", m=NP),
                                         ACT.Copy).then_inc(t_free[1] if causal else t_high, 1)

                def do(job, u):
                    name, j, n = job
                    if name == "proj":
                        drain(job, raw[:, n, :], lambda o: o[:, 0:NPROJ])
                    elif name == "gt":
                        drain(job, gT[0:3 * E, :], lambda o: o.bitcast(bf16)[0:3 * E, 0:S])
                    elif name == "pvb":
                        drain(job, o_low[:], lambda o: o[P:NP, :], done=o_half)

                if kind == FIRST:
                    for t in range(TT):
                        do(("proj", 0, t), None)
                else:
                    for u in range(HALF_U, UNITS):
                        if u + 1 < UNITS:
                            exps(u + 1, last_it)
                        for job in beside(kind, u):
                            do(job, u)
                        turned(u, last_it)
                if kind == TAIL:
                    for job in beside(kind, None):
                        do(job, None)
                    turned_out(b, NEXT, "aT", aT)
                    return
                act.wait_ge(qk_full, it * 2 + 1)
                for j in range(2):
                    last = nc.scalar.activation(q_s[0:P, j, :], sbank[0][j * P:(j + 1) * P, :], ACT.Copy)
                last.then_inc(qk_high, 1)
                act.wait_ge(qk_full, it * 2 + 2)
                for h in range(2):
                    for j in range(2):
                        last = nc.scalar.activation(k_h[h * P:(h + 1) * P, j, :], sbank[1][j * P:(j + 1) * P, :], ACT.Copy)
                last.then_inc(qk_high, 1)
                jobs = beside(kind, None)
                for job in jobs[:2] if kind == INNER else []:
                    do(job, None)
                for i in range(2):
                    act.wait_ge(stack_full, it * 2 + i + 1)
                    nc.scalar.activation(stackT[:, 2 * i:2 * i + 2, :], tbank[i].bitcast(bf16)[0:STK, :].rearrange("q (g s) -> q g s", g=2),
                                         ACT.Copy).then_inc(stack_out, 1)
                for job in jobs[2:] if kind == INNER else jobs:
                    do(job, None)
                if after_last:
                    roots(b * 3)
                exps(0, it)
                for u in range(HALF_U):
                    exps(u + 1, it)
                    for job in beside(kind, u):
                        do(job, u)
                    turned(u, it)

            def pairs(b):
                with act.Fori(1, HP) as p:
                    pair(b, p, INNER)
                pair(b, 0, TAIL)

            roots(0)
            turned_out(0, START, "xnT", xnT)
            gates_out(0, START)
            pair(0, 0, FIRST)
            with act.Fori(0, B - 1) as b:
                pairs(b)
                between(b, NEXT)
                pair(b + 1, 0, FIRST, after_last=True)
            pairs(B - 1)
            between(B - 1, END)
            roots(B * 3 - 1)

        @block.vector
        def _(dve):
            SSTEPS, BSTEPS, PSTEPS, LSTEPS = 21, 38, 30, 12
            dve.wait_ge(consts_in, 12 * 16)
            dve.wait_ge(zeroed, 3)
            for i, s in enumerate((v_ready, rope_ready, batch_done, out_stored, resid_ready)):
                nc.vector.memset(first_dve[:, i:i + 1], 0.0).then_inc(s, PRIME)
            base = nb = 0

            def made(ins):
                nonlocal nb
                nb += 1
                ins.then_inc(batch_step, 1)
                dve.wait_ge(batch_step, base + nb)

            def normalize(dst, src, n):
                for t in range(TT):
                    last = nc.vector.bn_stats(stats[:, t, :], src(t))
                made(last)
                nc.vector.memset(var[:], 0.0)
                for t in range(TT):
                    last = nc.vector.bn_aggr(mv[:, t, :], stats[:, t, :])
                made(last)
                nc.vector.tensor_scalar(var[:], mv[:, :, 1], EPS, None, ALU.add).then_inc(var_ready, 1)
                dve.wait_ge(root_ready, n + 1)
                made(nc.vector.reciprocal(rstd[:], root[:]))
                made(nc.vector.tensor_tensor(root[:], var[:], rstd[:], ALU.mult))
                made(nc.vector.tensor_tensor(root[:], root[:], rstd[:], ALU.mult))
                made(nc.vector.tensor_scalar(root[:], root[:], -0.5, 1.5, ALU.mult, ALU.add))
                made(nc.vector.tensor_tensor(rstd[:], rstd[:], root[:], ALU.mult))
                for t in range(TT):
                    last = nc.vector.tensor_scalar(dst[:, t, :], src(t), mv[:, t, 0:1], rstd[:, t:t + 1], ALU.subtract, ALU.mult)
                return last

            def row(i):
                return rows_sb[:, i:i + 1, :].to_broadcast([NP, TT, D])

            def norm_in(of, n):
                dve.wait_ge(x_in, of * 16 + 16)
                normalize(xn, lambda t: x_sb[:, t, :], n).then_inc(xn_ready, 1)

            def choose(b, kind, of):
                for i in range(TT // 2):
                    at = x_place(kind, ("gate", i))
                    dve.wait_ge(x_free[at % XB], b * (NX // XB) + 1 + at // XB + 1 + PRIME)
                if kind == NEXT:
                    dve.wait_ge(out_stored, b * 16 + PRIME)
                level = gate[:].rearrange("q t (g e) -> q (t g) e", e=E)
                one = pick[:].rearrange("q t (g e) -> q (t g) e", e=E)
                two = fin[:].rearrange("q t (g e) -> q (t g) e", e=E)
                top = best[:].rearrange("q t g -> q (t g)")
                wide = [NP, TT * 2 * H, E]
                top_b = top.unsqueeze(2).to_broadcast(wide)
                rank_b = rank_sb[:, None, :].to_broadcast(wide)
                made(nc.vector.tensor_scalar(gate[:], logit[:], SIG_ONE, None, ALU.min))
                for dst in (one, two):
                    made(nc.vector.tensor_reduce(top, level, AX.X, ALU.max))
                    made(nc.vector.tensor_tensor(dst, level, top_b, ALU.is_equal))
                    made(nc.vector.tensor_tensor(dst, dst, rank_b, ALU.mult))
                    made(nc.vector.tensor_reduce(top, dst, AX.X, ALU.max))
                    made(nc.vector.tensor_tensor(dst, dst, top_b, ALU.is_equal))
                    if dst is one:
                        made(nc.vector.scalar_tensor_tensor(gate[:], pick[:], -BIG, gate[:], ALU.mult, ALU.add))
                made(nc.vector.tensor_tensor(pick[:], pick[:], fin[:], ALU.add))
                dve.wait_ge(sig_ready, of + 1)
                made(nc.vector.tensor_tensor(gate[:], sig[:], pick[:], ALU.mult))
                nc.vector.memset(peak[:], 0.0)

            def x_sum(b, kind, name, dst, add):
                for i in range(TT // 2):
                    at = x_place(kind, (name, i))
                    dve.wait_ge(x_full, b * NX + XB + at + 1)
                    last = nc.vector.tensor_tensor(dst[:, 2 * i:2 * i + 2, :], xbank[at % XB][:].rearrange("q (t d) -> q t d", t=2), add[:, 2 * i:2 * i + 2, :], ALU.add)
                    last.then_inc(x_free[at % XB], 1)

            def between(b, kind):
                dve.wait_ge(o_done, b * (HP * 2 * EP) + HP * 2 * EP + PRIME)
                made(normalize(s1, lambda t: ybank[t // 2][:, (t % 2) * D:(t % 2 + 1) * D], b * 3 + (2 if kind == NEXT else 1)))
                made(nc.vector.tensor_tensor(s1[:], s1[:], row(0), ALU.mult))
                nc.vector.tensor_tensor(s1[:], s1[:], row(1), ALU.add).then_inc(s1_ready, 1)
                if kind == NEXT:
                    choose(b, kind, b + 1)
                dve.wait_ge(s1_ready, b + 1)
                dve.wait_ge(x_full, b * NX + XB + x_place(kind, ("s1T", 1)) + 1)
                made(nc.vector.tensor_tensor(s1[:], s1[:], row(4), ALU.add))
                assert kind == END or nb == BSTEPS - 7, nb

            def last_norm(b, kind):
                x_sum(b, kind, "f2", acc, s1)
                for i in range(TT // 2):
                    at = x_place(kind, ("f2", i))
                    dve.wait_ge(x_free[at % XB], b * (NX // XB) + 1 + at // XB + 1 + PRIME)
                normalize(acc, lambda t: acc[:, t, :], b * 3 + (3 if kind == NEXT else 2)).then_inc(acc_ready, 1)
                assert kind == END or nb == BSTEPS, nb

            def pair(b, p, kind, then=END, after_last=False):
                nonlocal base, nb
                it = b * HP + p
                last_it = it - 1 if kind == INNER else b * HP + (HP - 1)
                n_p = 0

                def step(ins):
                    nonlocal n_p
                    n_p += 1
                    ins.then_inc(dve_step, 1)
                    if kind == FIRST:
                        dve.wait_ge(dve_step, it * PSTEPS + n_p)
                    else:
                        dve.wait_ge(dve_step, last_it * PSTEPS + (PSTEPS - LSTEPS) + n_p)

                def w_filled(job):
                    at = place(kind, job)
                    dve.wait_ge(w_full, b * (HP * NJ) + p * NJ + at + 1 + PRIME)
                    return wbank[at % 2], w_free[at % 2]

                def w_read(job):
                    at = place(kind, job)
                    dve.wait_ge(w_free[at % 2], b * (HP * NJ // 2) + p * (NJ // 2) + at // 2 + 1 + PRIME)

                def v_gate(j, t):
                    o, free = w_filled(("v", j, t))
                    g = gates[:, t, 0, j * E:(j + 1) * E].unsqueeze(2).to_broadcast([NP, E, P])
                    nc.vector.tensor_tensor(vm[:, t % 2, :].rearrange("q (e c) -> q e c", e=E), o[:].rearrange("q (e c) -> q e c", e=E), g, ALU.mult).then_inc(free, 1)
                    w_read(("v", j, t))
                    nc.vector.tensor_reduce(v_sb[:, t, j, :], vm[:, t % 2, :].rearrange("q (e c) -> q c e", e=E), AX.X, ALU.add).then_inc(v_ready, 1)

                def row_peak(u, of):
                    j, qt, causal = unit(u)
                    dve.wait_ge(s_full, of * UNITS + u + 1)
                    step(nc.vector.tensor_reduce(peak[:, u:u + 1], sbank[u % 2][:, 0:(qt + 1) * NP if causal else S], AX.X, ALU.max))
                    nc.vector.tensor_scalar(bias[:, u:u + 1], peak[:, u:u + 1], -(CA ** -0.5 if causal else P ** -0.5), None, ALU.mult).then_inc(bias_ready, 1)

                def t_low(u, of):
                    qs = slice(unit(u)[1] * NP, (unit(u)[1] + 1) * NP)
                    dve.wait_ge(t_high, of * (UNITS // 2) + u // 2 + 1)
                    nc.vector.tensor_tensor(ptb_l[:, :, qs], tbank[0][:].rearrange("q (c m) -> q c m", m=NP), ptb_h.bitcast(f32)[:, :, qs], ALU.subtract).then_inc(t_free[0], 1)

                def gate_parts(j, of):
                    dve.wait_ge(exp_done, of * UNITS + 8 * j + 7 + PRIME)
                    step(nc.vector.reciprocal(rden[:, j, 0, :], den[:, j, 0, :]))
                    step(nc.vector.tensor_tensor(gs[:, j, 0], gates[:, :, 1, j * E:(j + 1) * E], rden[:, j, 0, :].unsqueeze(2).to_broadcast([NP, TT, E]), ALU.mult))
                    step(nc.vector.tensor_copy(gpart[:, j, :, 0, :], gs[:, j, 0]))
                    step(nc.vector.tensor_tensor(gs[:, j, 1], gs[:, j, 0], gpart[:, j, :, 0, :], ALU.subtract))
                    step(nc.vector.tensor_copy(gpart[:, j, :, 1, :], gs[:, j, 1]))
                    nc.vector.tensor_tensor(gpart[:, j, :, 2, :], gs[:, j, 1], gpart[:, j, :, 1, :], ALU.subtract).then_inc(gpart_ready, 1)

                def a_rows(j):
                    o, free = w_filled(("pva", j, 0))
                    at = (HP - 1) * 2 * CA + j * CA if kind == TAIL else p * (2 * CA) + (j - 2) * CA
                    nc.vector.tensor_tensor(a_sb[:, :, bass.ds(at, CA)], o[:, 0:TT * CA].rearrange("q (t c) -> q t c", t=TT),
                                            rden[:, j, 1, :].unsqueeze(2).to_broadcast([NP, TT, CA]), ALU.mult).then_inc(free, 1)

                def o_sum(j, of):
                    o, free = w_filled(("pvb", j, 0))
                    dve.wait_ge(o_half, of * 2 + j + 1)
                    nc.vector.tensor_tensor(oT[0:P, :], o[0:P, :], o_low[:], ALU.add)
                    nc.vector.tensor_tensor(oT[P:NP, :], o[0:P, :], o_low[:], ALU.add).then_inc(free, 1)

                def u_gate(j, e, of):
                    if e == 0:
                        at = place_done(kind, ("pvb", j, 0))
                        dve.wait_ge(w_free[at % 2], b * (HP * NJ // 2) + p * (NJ // 2) + at // 2 + 1 + PRIME)
                    o, free = w_filled(("g", j, e))
                    dve.wait_ge(o_done, of * (2 * EP) + j * EP + e - 1 + PRIME)
                    nc.vector.tensor_tensor(u_sb[:, e % 2, :], o[:], oT[:], ALU.mult).then_inc(free, 1)

                def rotate():
                    for t in (TT - 2, TT - 1):
                        w_read(("proj", 0, t))
                    head = raw[:, :, 0:NQK].rearrange("q t (g c) -> q t g c", g=4)
                    a, c = head[:, :, :, 0:HALF], head[:, :, :, HALF:NROT]
                    cos = rope_sb[:, 0].unsqueeze(2).to_broadcast([NP, TT, 4, HALF])
                    sin = rope_sb[:, 1].unsqueeze(2).to_broadcast([NP, TT, 4, HALF])
                    nc.vector.tensor_tensor(rot[:, 0], a, cos, ALU.mult)
                    nc.vector.tensor_tensor(rot[:, 1], c, sin, ALU.mult)
                    nc.vector.tensor_tensor(rot[:, 2], a, sin, ALU.mult)
                    step(nc.vector.tensor_tensor(rot[:, 3], c, cos, ALU.mult))
                    nc.vector.tensor_tensor(a, rot[:, 0], rot[:, 1], ALU.subtract)
                    nc.vector.tensor_tensor(c, rot[:, 2], rot[:, 3], ALU.add).then_inc(rope_ready, 1)

                def do(job, u):
                    name, j, n = job
                    of = last_it if of_last(job, u) else it
                    if name == "v":
                        v_gate(j, n)
                    elif name == "pvb":
                        o_sum(j, of)
                    elif name == "pva":
                        a_rows(j)
                    elif name == "g":
                        u_gate(j, n, of)

                def tiles(units, of, end):
                    for u in units:
                        if u == 7:
                            t_low(u - 1, of)
                        if u + 1 < end:
                            row_peak(u + 1, of)
                        if unit(u)[2] and u != 7:
                            t_low(u - 1, of)
                        for job in beside(kind, u):
                            do(job, u)
                        if u % 8 == 6:
                            gate_parts(u // 8, of)
                        elif u % 8 == 7:
                            dve.wait_ge(exp_done, of * UNITS + u + 1 + PRIME)
                            step(nc.vector.reciprocal(rden[:, u // 8, 1, :], den[:, u // 8, 1, :]))
                        if u == UNITS - 2 and kind == INNER:
                            rotate()

                if kind == FIRST:
                    rotate()
                else:
                    tiles(range(HALF_U, UNITS), last_it, UNITS)
                    assert n_p == LSTEPS + (kind == INNER), n_p
                if kind == TAIL:
                    for job in beside(kind, None):
                        do(job, None)
                    dve.wait_ge(batch_done, b + PRIME)
                    x_sum(b, NEXT, "wo", resid, x_sb)
                    for i in range(TT // 2):
                        at = x_place(NEXT, ("wo", i))
                        dve.wait_ge(x_free[at % XB], b * (NX // XB) + 1 + at // XB + 1 + PRIME)
                    nc.vector.memset(peak[:], 0.0).then_inc(resid_ready, 1)
                    for u in range(HALF_U):
                        for job in beside(kind, u):
                            do(job, u)
                    base, nb = SSTEPS + b * BSTEPS, 0
                    if then == NEXT:
                        norm_in(b + 1, b * 3 + 1)
                    return
                step(nc.vector.tensor_copy(gates[:], gate[:].rearrange("q t (v n) -> q t v n", v=2)[:, :, :, bass.ds(p * G2, G2)]))
                dve.wait_ge(qk_high, it * 2 + 1)
                for j in range(2):
                    last = nc.vector.tensor_tensor(q_s[P:NP, j, :], sbank[0][j * P:(j + 1) * P, :], q_s.bitcast(f32)[0:P, j, :], ALU.subtract)
                last.then_inc(qk_low, 1)
                dve.wait_ge(qk_high, it * 2 + 2)
                for h in range(2):
                    for j in range(2):
                        last = nc.vector.tensor_tensor(k_l[h * P:(h + 1) * P, j, :], sbank[1][j * P:(j + 1) * P, :], k_h.bitcast(f32)[0:P, j, :], ALU.subtract)
                last.then_inc(qk_low, 1)
                if after_last:
                    last_norm(b - 1, NEXT)
                for job in beside(kind, None):
                    do(job, None)
                row_peak(0, it)
                tiles(range(HALF_U), it, UNITS)
                assert n_p == (PSTEPS - LSTEPS if kind == FIRST else PSTEPS), n_p

            def pairs(b, then):
                with dve.Fori(1, HP) as p:
                    pair(b, p, INNER)
                pair(b, 0, TAIL, then)

            norm_in(0, 0)
            choose(0, START, 0)
            assert nb == SSTEPS, nb
            pair(0, 0, FIRST)
            with dve.Fori(0, B - 1) as b:
                pairs(b, NEXT)
                between(b, NEXT)
                pair(b + 1, 0, FIRST, after_last=True)
            pairs(B - 1, END)
            between(B - 1, END)
            last_norm(B - 1, END)


def kernel(**inputs):
    import ml_dtypes
    import numpy as np
    import concourse.bacc as bacc
    from concourse import mybir as mb
    from concourse.bass_utils import run_bass_kernel_spmd

    a = {k: np.asarray(v) for k, v in inputs.items()}

    def chunks(w):
        return np.ascontiguousarray(w.reshape(-1, NP, w.shape[1]).transpose(1, 0, 2))

    f = "L0_ffn_"
    cols = []
    for h in range(0, H, 2):
        cols.append(np.concatenate(
            [a[f + "Wq"][h], a[f + "Wq"][h + 1], a[f + "Wk"][h], a[f + "Wk"][h + 1]]
            + [a["L0_attn_" + w][:, h * CA:(h + 2) * CA] for w in ("WQ", "WK", "WV")], axis=1))
    wqk = np.stack([chunks(c) for c in cols])
    wv = np.stack([chunks(a[f + "Wv"][h:h + 2].transpose(2, 0, 1, 3).reshape(D, 2 * E * P)) for h in range(0, H, 2)])
    wo = np.stack([chunks(a[f + "Wo"][h:h + 2].reshape(2 * E * P, D)) for h in range(0, H, 2)])
    wsel = chunks(np.concatenate([a[f + "Wsel_v"].reshape(H * E, D), a[f + "Wsel_o"].reshape(H * E, D)]).T)
    rows = np.stack([a[f + n] for n in ("ln1_g", "ln1_b", "ln2_g", "ln2_b", "b2")])
    rows = np.ascontiguousarray(np.broadcast_to(rows, (NP, 5, D)))
    inv = np.float32(10000.0) ** (-np.arange(HALF, dtype=np.float32) / np.float32(HALF))
    ang = np.arange(S, dtype=np.float32)[:, None] * inv[None, :]
    rope = np.stack([np.cos(ang), np.sin(ang)]).astype(np.float32).reshape(2, TT, NP, HALF).transpose(2, 0, 1, 3)
    bf = ml_dtypes.bfloat16
    mask = np.where(np.arange(NP)[None, :] > np.arange(NP)[:, None], -BIG, 0.0).astype(bf)
    sel = np.zeros((NP, EP, NP), bf)
    for s in range(3):
        for e in range(E):
            sel[s * E + e, e // 2, (e % 2) * P:(e % 2 + 1) * P] = 1
    rank = np.broadcast_to(np.arange(E, 0, -1, dtype=np.float32), (NP, E))
    arrays = {
        "x": a["L0_attn_x"], "wqk": wqk, "wv": wv, "wo": wo, "wsel": wsel, "w_out": chunks(a["L0_attn_WO"]),
        "w1": chunks(a[f + "W1"]), "w2": chunks(a[f + "W2"]), "b1": np.ascontiguousarray(a[f + "b1"].reshape(FC, NP).T),
        "rows": rows, "ident": np.eye(NP, dtype=np.float32), "ident_h": np.eye(NP).astype(bf), "mask": mask, "sel": sel,
        "rope": rope, "rank": rank,
    }
    arrays = {k: np.ascontiguousarray(v) for k, v in arrays.items()}
    nc = bacc.Bacc("TRN2", target_bir_lowering=False, num_devices=1)
    args = [nc.dram_tensor("in_" + k, v.shape, mb.dt.from_np(v.dtype), kind="ExternalInput").ap() for k, v in arrays.items()]
    out = nc.dram_tensor("out", (B, S, D), mb.dt.float32, kind="ExternalOutput").ap()
    build(nc, *args, out)
    r = run_bass_kernel_spmd(nc, [{"in_" + k: v for k, v in arrays.items()}], core_ids=[0])
    return r.results[0]["out"]
```
